# Optimizing a Trainium2 kernel written in Bass

```python
import numpy as np
import jax
import jax.numpy as jnp

def _softmax(x, axis=-1):
    return jax.nn.softmax(x, axis=axis)

def _gelu(x):
    return jax.nn.gelu(x, approximate=True)

def _silu(x):
    return jax.nn.silu(x)

def _sigmoid(x):
    return jax.nn.sigmoid(x)

def _layernorm(x, axis=-1, eps=1e-05):
    m = jnp.mean(x, axis=axis, keepdims=True)
    v = jnp.var(x, axis=axis, keepdims=True)
    return (x - m) / jnp.sqrt(v + eps)

def _scatter_add(tgt, idx, src, axis=0):
    return tgt.at[idx].add(src)

def _segment_sum(src, seg, n):
    return jax.ops.segment_sum(src, seg, n)
kernel_name = 'mk_gnn_preln_d2_gnn_r8_19093b'

def setup_inputs(seed: int=0):
    np.random.seed(seed)
    _w = jnp.asarray

    def _rec_inputs():
        import jax
        import jax.numpy as jnp
        _gk = jax.random.key(seed)
        x = -0.0008691 + 1 * jax.random.normal(jax.random.fold_in(_gk, 1), (12500, 128), jnp.float32)
        _s = jax.random.randint(jax.random.fold_in(_gk, 2), (200000,), 0, 12500, jnp.int32)
        _d = jax.random.randint(jax.random.fold_in(_gk, 3), (200000,), 0, 12500, jnp.int32)
        _loop = jnp.arange(12500, dtype=jnp.int32)
        src = jnp.concatenate([_s, _d, _loop])
        dst = jnp.concatenate([_d, _s, _loop])
        _o = jnp.argsort(dst, stable=True)
        src = src[_o]
        dst = dst[_o]
        edge_type_2 = jax.random.randint(jax.random.fold_in(_gk, 13), (412500,), 0, 2, jnp.int32)
        return (x, src, dst, edge_type_2)
    x, src, dst, edge_type_2 = _rec_inputs()

    def _L0_gnn_setup():
        import jax, jax.numpy as jnp
        import numpy as np
        IN_DIM = 128
        OUT_DIM = 128
        N_NODES = 1250
        N_EDGES = 80000
        key = jax.random.key(seed)
        ks = jax.random.split(key, 9)
        X = jax.random.normal(ks[0], (N_NODES, IN_DIM), dtype=jnp.float32)
        edge_index = jax.random.randint(ks[1], (2, N_EDGES), 0, N_NODES, dtype=jnp.int64)
        edge_types = jax.random.randint(ks[2], (N_EDGES,), 0, 2, dtype=jnp.int64)
        s = 1.0 / np.sqrt(IN_DIM)
        W_data = jax.random.uniform(ks[3], (OUT_DIM, IN_DIM), minval=-s, maxval=s, dtype=jnp.float32)
        b_data = jax.random.uniform(ks[4], (OUT_DIM,), minval=-s, maxval=s, dtype=jnp.float32)
        W_control = jax.random.uniform(ks[5], (OUT_DIM, IN_DIM), minval=-s, maxval=s, dtype=jnp.float32)
        b_control = jax.random.uniform(ks[6], (OUT_DIM,), minval=-s, maxval=s, dtype=jnp.float32)
        W_self = jax.random.uniform(ks[7], (OUT_DIM, IN_DIM), minval=-s, maxval=s, dtype=jnp.float32)
        b_self = jax.random.uniform(ks[8], (OUT_DIM,), minval=-s, maxval=s, dtype=jnp.float32)
        return {'X': X, 'edge_index': edge_index, 'edge_types': edge_types, 'W_data': W_data, 'b_data': b_data, 'W_control': W_control, 'b_control': b_control, 'W_self': W_self, 'b_self': b_self}
    _L0_gnn_all = _L0_gnn_setup()
    _L0_gnn_in = {k: v for k, v in _L0_gnn_all.items() if k in ('W_data', 'b_data', 'W_control', 'b_control', 'W_self', 'b_self')}
    del _L0_gnn_all

    def _L1_gnn_setup():
        import jax, jax.numpy as jnp
        import numpy as np
        N_NODES = 12500
        N_EDGES = 400000
        IN_DIM = 128
        OUT_DIM = 128
        key = jax.random.key(seed)
        k1, k2, k3, k4, k5 = jax.random.split(key, 5)
        h = jax.random.normal(k1, (N_NODES, IN_DIM), dtype=jnp.float32)
        W_in = jax.random.normal(k2, (OUT_DIM, IN_DIM), dtype=jnp.float32) * 0.05
        W_out = jax.random.normal(k3, (OUT_DIM, IN_DIM), dtype=jnp.float32) * 0.05
        src = jax.random.randint(k4, (N_EDGES,), 0, N_NODES, dtype=jnp.int32)
        dst = jax.random.randint(k5, (N_EDGES,), 0, N_NODES, dtype=jnp.int32)
        return {'h': h, 'W_in': W_in, 'W_out': W_out, 'src': src, 'dst': dst}
    _L1_gnn_all = _L1_gnn_setup()
    _L1_gnn_in = {k: v for k, v in _L1_gnn_all.items() if k in ('W_in', 'W_out')}
    del _L1_gnn_all
    return {'x': x, 'src': src, 'dst': dst, 'edge_type_2': edge_type_2, 'L0_gnn_W_data': _L0_gnn_in['W_data'], 'L0_gnn_b_data': _L0_gnn_in['b_data'], 'L0_gnn_W_control': _L0_gnn_in['W_control'], 'L0_gnn_b_control': _L0_gnn_in['b_control'], 'L0_gnn_W_self': _L0_gnn_in['W_self'], 'L0_gnn_b_self': _L0_gnn_in['b_self'], 'L1_gnn_W_in': _L1_gnn_in['W_in'], 'L1_gnn_W_out': _L1_gnn_in['W_out']}

def reference(x, src, dst, edge_type_2, L0_gnn_W_data, L0_gnn_b_data, L0_gnn_W_control, L0_gnn_b_control, L0_gnn_W_self, L0_gnn_b_self, L1_gnn_W_in, L1_gnn_W_out):
    import jax
    import jax.numpy as jnp

    def _L0_gnn_ref(X, edge_index, edge_types, W_data, b_data, W_control, b_control, W_self, b_self):
        import jax, jax.numpy as jnp
        import numpy as np
        IN_DIM = 128
        OUT_DIM = 128
        N_NODES = 1250
        N_EDGES = 80000
        src, dst = (edge_index[0], edge_index[1])
        Xs = X[src]
        m_data = Xs @ W_data.T + b_data
        m_ctrl = Xs @ W_control.T + b_control
        msg = jnp.where((edge_types == 0)[:, None], m_data, m_ctrl)
        agg = jax.ops.segment_sum(msg, dst, num_segments=X.shape[0])
        out = agg + (X @ W_self.T + b_self)
        return jax.nn.relu(out)

    def _L1_gnn_ref(h, W_in, W_out, src, dst):
        import jax, jax.numpy as jnp
        import numpy as np
        N_NODES = 12500
        N_EDGES = 400000
        IN_DIM = 128
        OUT_DIM = 128
        n = h.shape[0]
        z_in = h @ W_in.T
        z_out = h @ W_out.T
        agg = jax.ops.segment_sum(z_in[src], dst, num_segments=n)
        deg = jax.ops.segment_sum(jnp.ones_like(dst, dtype=h.dtype), dst, num_segments=n)
        return agg + deg[:, None] * z_out
    edge_index = jnp.stack([src, dst])
    h = jnp.maximum(_layernorm(x, axis=-1), 0.0)
    x = x + _L0_gnn_ref(h, edge_index, edge_type_2, L0_gnn_W_data, L0_gnn_b_data, L0_gnn_W_control, L0_gnn_b_control, L0_gnn_W_self, L0_gnn_b_self)
    h = jnp.maximum(_layernorm(x, axis=-1), 0.0)
    x = x + _L1_gnn_ref(h, L1_gnn_W_in, L1_gnn_W_out, src, dst)
    return x

_drawn_inputs = setup_inputs


def setup_inputs(seed=0):
    import zlib

    import numpy as np

    out = dict(_drawn_inputs(seed))
    spreads = {}
    factors = {'L0_gnn_b_self': 4.454}
    for name, (base, spread) in spreads.items():
        noise = np.random.default_rng([zlib.crc32(name.encode()), seed]).standard_normal(out[name].shape)
        drawn = base * np.exp(spread * noise) if base else spread * noise
        out[name] = jnp.asarray(drawn.astype(out[name].dtype))
    for name, factor in factors.items():
        out[name] = (out[name] * factor).astype(out[name].dtype)
    return out
```

```python
import concourse.bass as bass
from concourse import mybir
from contextlib import ExitStack

P = 128



def gnn_kernel(nc, x, src, dst, etype, w_data, b_data, w_ctrl, b_ctrl, w_self, b_self, w_in, w_out, out):
    fp32, bf16, i32 = mybir.dt.float32, mybir.dt.bfloat16, mybir.dt.int32
    ALU, ACT = mybir.AluOpType, mybir.ActivationFunctionType
    EPS = 1e-5

    N, F = x.shape
    E = src.shape[0]
    assert F == P
    NB = -(-N // P)
    LAST = N - (NB - 1) * P
    TPB = -(-E // N)
    T = NB * TPB
    assert NB % 2 == 0 and NB >= 4 and T * P >= E
    NPAD = NB * P
    HALVES = ((0, (TPB + 1) // 2), ((TPB + 1) // 2, TPB))
    TA = HALVES[0][1]
    PARTS = 3
    RW = PARTS * F
    RC = RW + 1
    RS = RC + 1
    W2 = 2 * P

    CH = -(-T // P)
    FULL = E // P
    REM = E - FULL * P
    FCH = FULL // P
    XTRA = FULL - FCH * P
    PADS = T * P - E
    EDGE_LOADS = 16 * 3 * ((FCH > 0) + (XTRA > 0) + (REM > 0))

    table0 = nc.dram_tensor("table0", (2 * NPAD, RW), bf16, kind="Internal").ap()
    table1 = nc.dram_tensor("table1", (NPAD, RW), bf16, kind="Internal").ap()
    table0_blocks = table0.rearrange("(t q) c -> q t c", t=2)

    ctx = ExitStack()
    with ctx:
        def sb(name, shape, dt):
            return ctx.enter_context(nc.sbuf_tensor(name, shape, dt))

        def pb(name, shape, dt=fp32):
            return ctx.enter_context(nc.psum_tensor(name, shape, dt))

        def sem(name):
            return ctx.enter_context(nc.semaphore(name))

        x_sb = sb("x_sb", [P, NB * F], fp32)
        own = sb("own", [P, NB * F], fp32)
        idx0 = sb("idx0", [P, T], fp32)
        idx1 = sb("idx1", [P, T], fp32)
        dst_f = sb("dst_f", [P, T], fp32)
        row_words = TPB * RS // 2 + (TPB * RS) % 2
        hot_words = TPB * W2 // 2
        arena_words = max(row_words + hot_words, 3 * CH * P)
        arena = sb("arena", [P, arena_words], fp32)
        rows = arena[:, 0:row_words].bitcast(bf16)[:, 0:TPB * RS].rearrange("p (t c) -> p t c", c=RS)
        hot = arena[:, row_words:row_words + hot_words].bitcast(bf16).rearrange("p (t c) -> p t c", c=W2)
        raw = [arena[:, a * CH * P:(a + 1) * CH * P] for a in range(3)]
        raw_i = [r.bitcast(i32) for r in raw]

        idx_now = sb("idx_now", [P, 2, TPB], i32)
        base = sb("base", [P, TPB], fp32)
        base_i = sb("base_i", [P, TPB], i32)
        rel = sb("rel", [P, TPB], fp32)
        bases_i = own[:, 0:T].bitcast(i32)
        bases = own[:, T:2 * T]
        ident = sb("ident", [P, P], fp32)
        ones = sb("ones", [P, 1], fp32)
        zeros = sb("zeros", [P, RC], bf16)
        eps = sb("eps", [P, 1], fp32)
        iota_i = sb("iota_i", [P, W2], i32)
        w_raw = sb("w_raw", [P, 5, F], fp32)
        wT = sb("wT", [P, 5, F], fp32)
        bias = sb("bias", [P, 3, F], fp32)
        stats = sb("stats", [P, NB * 6], fp32)
        mean2 = sb("mean2", [P, NB], fp32)
        var = sb("var", [P, NB], fp32)
        std = sb("std", [P, NB], fp32)
        rstd = sb("rstd", [P, NB], fp32)
        shift = sb("shift", [P, NB], fp32)

        def stat_col(c):
            return stats[:, :].rearrange("p (n c) -> p n c", c=6)[:, :, c]
        missed = sb("missed", [P, 1], fp32)
        covered = sb("covered", [1, 1], i32)
        xn = sb("xn", [P, 2, F], fp32)
        hT = sb("hT", [P, 2, P], fp32)
        y = sb("y", [P, 2, 2, F], fp32)
        rest = sb("rest", [P, 2, 2, F], fp32)
        row_out = sb("row_out", [P, 2, 2, PARTS, F], bf16)
        agg = sb("agg", [P, RC], fp32)
        low = sb("low", [P, F], fp32)
        tot = sb("tot", [P, F], fp32)
        res = sb("res", [P, 2, F], fp32)
        st1 = sb("st1", [P, 6], fp32)
        mv1 = sb("mv1", [P, 2], fp32)
        std1 = sb("std1", [P, 1], fp32)
        rstd1 = sb("rstd1", [P, 1], fp32)

        bank = [pb(f"bank{k}", [P, 512]) for k in range(2)]
        psT = [pb(f"psT{k}", [P, 512]) for k in range(2)]
        psZ = [pb(f"psZ{k}", [P, 512]) for k in range(2)]
        iota_ps = pb("iota_ps", [P, 512])
        psM = pb("psM", [P, 512])

        def blk(t, n):
            return t[:, bass.ds(n * F, F)]

        s_edges = sem("s_edges")
        s_w = sem("s_w")
        s_x = sem("s_x")
        s_pads = sem("s_pads")
        s_const = sem("s_const")
        s_ident = sem("s_ident")
        s_float = sem("s_float")
        s_tr = sem("s_tr")
        s_trc = sem("s_trc")
        s_wt = sem("s_wt")
        s_wtc = sem("s_wtc")
        s_iota = sem("s_iota")
        s_bn = sem("s_bn")
        s_rstd = sem("s_rstd")
        s_idx0 = sem("s_idx0")
        s_far = sem("s_far")
        s_yab = sem("s_yab")
        s_bases = sem("s_bases")
        s_missed = sem("s_missed")
        s_missum = sem("s_missum")
        s_covered = sem("s_covered")
        s_var = sem("s_var")
        s_mean = sem("s_mean")
        s_std = sem("s_std")
        s_shift = sem("s_shift")
        s_xn = sem("s_xn")
        s_xnT = sem("s_xnT")
        s_hT = sem("s_hT")
        s_z = sem("s_z")
        s_y = sem("s_y")
        s_hi = sem("s_hi")
        s_rest = sem("s_rest")
        s_mid = sem("s_mid")
        s_low = sem("s_low")
        s_rfree = sem("s_rfree")
        s_own = sem("s_own")
        s_st0 = [sem(f"s_st0{k}") for k in range(2)]
        s_st1 = [sem(f"s_st1{k}") for k in range(2)]
        s_out = [sem(f"s_out{k}") for k in range(2)]
        s_one = sem("s_one")

        class Layer:
            pass

        L = []
        for l in range(2):
            s = Layer()
            s.staged = sem(f"l{l}_staged")
            s.gathered = [sem(f"l{l}_gathered{h}") for h in "AB"]
            s.based = sem(f"l{l}_based")
            s.rel = sem(f"l{l}_rel")
            s.hot = [sem(f"l{l}_hot{h}") for h in "AB"]
            s.used = [sem(f"l{l}_used{h}") for h in "AB"]
            s.evac = sem(f"l{l}_evac")
            s.agg_free = sem(f"l{l}_agg_free")
            s.low = sem(f"l{l}_low")
            s.tot = sem(f"l{l}_tot")
            s.x = sem(f"l{l}_x")
            s.bn = sem(f"l{l}_bn")
            s.var = sem(f"l{l}_var")
            s.std = sem(f"l{l}_std")
            s.rstd = sem(f"l{l}_rstd")
            s.xn = sem(f"l{l}_xn")
            s.xnT = sem(f"l{l}_xnT")
            s.hT = sem(f"l{l}_hT")
            s.z = sem(f"l{l}_z")
            s.hi = sem(f"l{l}_hi")
            s.rest = sem(f"l{l}_rest")
            s.mid = sem(f"l{l}_mid")
            s.ready = sem(f"l{l}_ready")
            s.rfree = sem(f"l{l}_rfree")
            s.own = sem(f"l{l}_own")
            L.append(s)

        s_apart = {nc.gpsimd.engine: sem("s_apart_pool"), nc.vector.engine: sem("s_apart_dve")}

        block = ctx.enter_context(nc.Block())

        def in_pairs(eng, step):
            with eng.Fori(0, NB // 2 - 1) as i:
                for k in range(2):
                    step(i * 2 + k, k)
            for k in range(2):
                step(NB - 2 + k, k)

        def is_there(n):
            return not isinstance(n, int) or n < NB

        def wait_apart(eng, semaphore, n):
            eng.wait_ge(semaphore, n)
            eng.sem_inc(s_apart[eng.engine], 1)

        def either_path(eng, fast, general):
            eng.wait_ge(s_covered, 1)
            with eng.If(eng.value_load(covered[0:1, 0:1], min_val=0, max_val=1) == 1):
                fast()
            with eng.Else():
                general()

        @block.sync
        def _(sp):
            sp.sem_inc(s_rfree, 2)
            for l in range(2):
                sp.sem_inc(L[l].rfree, 2)
            sp.wait_ge(s_pads, 4)
            for a, lst in enumerate((dst, src, etype)):
                if FCH:
                    sp.dma_start(raw_i[a][:, 0:FCH * P].rearrange("p (c e) -> p c e", e=P),
                                 lst[0:FCH * P * P].rearrange("(c p e) -> p c e", p=P, e=P)).then_inc(s_edges, 16)
                if XTRA:
                    sp.dma_start(raw_i[a][0:XTRA, FCH * P:FCH * P + P],
                                 lst[FCH * P * P:FULL * P].rearrange("(p e) -> p e", e=P)).then_inc(s_edges, 16)
                if REM:
                    sp.dma_start(raw_i[a][XTRA:XTRA + 1, FCH * P:FCH * P + REM],
                                 lst[FULL * P:E].rearrange("(p e) -> p e", p=1)).then_inc(s_edges, 16)
            x_view = x[0:(NB - 1) * P, :].rearrange("(n p) f -> p n f", p=P)
            sp.dma_start(x_sb[:, 0:(NB - 1) * F].rearrange("p (n f) -> p n f", f=F), x_view).then_inc(s_x, 16)
            sp.dma_start(x_sb[0:LAST, (NB - 1) * F:NB * F], x[(NB - 1) * P:N, :]).then_inc(s_x, 16)

            def store0(n, k):
                sp.wait_ge(s_low, n + 1)
                sp.dma_start(table0_blocks[bass.ds(n * P, P), :, :],
                             row_out[:, k, :, :, :].rearrange("p t a f -> p t (a f)")).then_inc(s_st0[k], 16)
                if k == 1:
                    for j in range(2):
                        sp.wait_ge(s_st0[j], (n - 1) * 8 + 16)
                        sp.sem_inc(s_rfree, 1)
            in_pairs(sp, store0)

            def store(l, m, k):
                s = L[l]
                sp.wait_ge(s.ready, m + 1)
                done = (s_st1, s_out)[l]
                if l == 0:
                    sp.dma_start(table1[bass.ds(m * P, P), :],
                                 row_out[:, k, 0, :, :].rearrange("p a f -> p (a f)")).then_inc(done[k], 16)
                elif isinstance(m, int) and m == NB - 1:
                    sp.dma_start(out[m * P:N, :], res[0:LAST, k, :]).then_inc(done[k], 16)
                else:
                    sp.dma_start(out[bass.ds(m * P, P), :], res[:, k, :]).then_inc(done[k], 16)
                if k == 1:
                    for j in range(2):
                        sp.wait_ge(done[j], (m - 1) * 8 + 16)
                        sp.sem_inc(s.rfree, 1)

            for l in range(2):
                in_pairs(sp, lambda m, k: store(l, m, k))
            for k in range(2):
                sp.wait_ge(s_out[k], 16 * (NB // 2))

        @block.gpsimd
        def _(pool):
            for a, v in enumerate((-1, 0, 0)):
                pool.memset(raw_i[a][:, FCH * P:CH * P], v).then_inc(s_pads, 1)
            pool.memset(x_sb[:, (NB - 1) * F:NB * F], 0.0).then_inc(s_pads, 1)
            pool.memset(ident[:, :], 0.0).then_inc(s_ident, 1)
            pool.memset(ones[:, :], 1.0).then_inc(s_const, 1)
            pool.memset(zeros[:, :], 0.0).then_inc(s_const, 1)
            pool.memset(eps[:, :], EPS).then_inc(s_const, 1)
            pool.wait_ge(s_ident, 1)
            pool.affine_select(out=ident[:, :], in_=ident[:, :], compare_op=ALU.not_equal, fill=1.0,
                               base=0, pattern=[[-1, P]], channel_multiplier=1).then_inc(s_ident, 1)
            pool.iota(iota_i[:, :], [[1, W2]], base=0, channel_multiplier=0).then_inc(s_const, 1)
            for h, (a, b) in enumerate(HALVES):
                pool.iota(base_i[:, a:b], [[0, b - a]], base=(h - 1) * P, channel_multiplier=0).then_inc(s_const, 1)
                pool.iota(bases_i.rearrange("p (n t) -> p n t", t=TPB)[:, :, a:b], [[P, NB], [0, b - a]],
                          base=(h - 1) * P, channel_multiplier=0).then_inc(s_bases, 1)
            pool.wait_ge(s_edges, EDGE_LOADS)
            for a in (1, 2):
                pool.tensor_copy(raw[a], raw_i[a]).then_inc(s_float, 1)

            def split(n, k):
                pool.wait_ge(s_hi, n + 1)
                pool.tensor_tensor(rest[:, k, :, :], y[:, k, :, :], row_out[:, k, :, 0, :],
                                   op=ALU.subtract).then_inc(s_rest, 1)
                pool.wait_ge(s_mid, n + 1)
                pool.tensor_tensor(row_out[:, k, :, 2, :], rest[:, k, :, :], row_out[:, k, :, 1, :],
                                   op=ALU.subtract).then_inc(s_low, 1)
            in_pairs(pool, split)
            for k in range(2):
                pool.wait_ge(s_st0[k], 16 * (NB // 2))

            def gather(l, seq, k):
                s = L[l]
                wait_apart(pool, s.staged, seq + 1)
                for h, (a, b) in enumerate(HALVES):
                    wait_apart(pool, s.used[h], seq + 1 + h)
                    for t in range(a, b):
                        pool.indirect_dma_start(
                            out=rows[:, t, 0:RW], out_offset=None, in_=(table0, table1)[l],
                            in_offset=bass.IndirectOffsetOnAxis(ap=idx_now[:, k, t:t + 1], axis=0),
                            compute_op=ALU.bypass).then_inc(s.gathered[h], 16)

            def gather_general(l):
                with pool.Fori(0, NB // 2) as g:
                    with pool.Fori(0, NB // 2) as i:
                        for k in range(2):
                            gather(l, g * NB + i * 2 + k, k)

            for l in range(2):
                if l == 1:
                    for k in range(2):
                        pool.wait_ge(s_st1[k], 16 * (NB // 2))
                either_path(pool, lambda: in_pairs(pool, lambda n, k: gather(l, n, k)), lambda: gather_general(l))

        @block.tensor
        def _(pe):
            pe.wait_ge(s_ident, 2)
            pe.wait_ge(s_w, 16 * 8)
            for j in range(5):
                pe.transpose((psT + psZ + bank)[j][:, 0:P], w_raw[:, j, :], ident[:, :]).then_inc(s_wt, 1)
            pe.wait_ge(s_float, 3)
            pe.wait_ge(s_wtc, 5)
            g = 0
            for a in range(3):
                for c0 in range(0, CH, 4):
                    if g >= 4:
                        pe.wait_ge(s_trc, g - 3)
                    for c in range(c0, min(c0 + 4, CH)):
                        last = pe.transpose((psT + psZ)[g % 4][:, (c - c0) * P:(c - c0 + 1) * P],
                                            raw[a][:, c * P:(c + 1) * P], ident[:, :])
                    last.then_inc(s_tr, 1)
                    g += 1
            pe.wait_ge(s_trc, g)

            def multiply(n, k):
                pe.wait_ge(s_hT, n + 1)
                pe.wait_ge(s_y, n + 1)
                pe.matmul(psZ[k][:, 0:3 * F], hT[:, k, :], wT[:, 0:3, :].rearrange("p j f -> p (j f)"),
                          start=True, stop=True).then_inc(s_z, 1)
                if is_there(n + 2):
                    pe.wait_ge(s_xn, n + 3)
                    pe.transpose(psT[k][:, 0:P], xn[:, k, :], ident[:, :]).then_inc(s_xnT, 1)
            for k in range(2):
                pe.wait_ge(s_xn, k + 1)
                pe.transpose(psT[k][:, 0:P], xn[:, k, :], ident[:, :]).then_inc(s_xnT, 1)
            in_pairs(pe, multiply)
            pe.wait_ge(s_missed, 1)
            pe.matmul(psM[0:1, 0:1], missed[:, :], ones[:, :], start=True, stop=True).then_inc(s_missum, 1)

            def add_rows(l, seq, h, to, fresh=None):
                s = L[l]
                pe.wait_ge(s.hot[h], seq + 2 if h else seq + 1)
                if fresh is not None:
                    pe.wait_ge(s.evac, fresh)
                a, b = HALVES[h]
                pe.wait_ge(s.gathered[h], (seq + 1) * (16 * (b - a)))
                for t in range(a, b):
                    for w in range(2):
                        last = pe.matmul(bank[to[w]][:, 0:RC], hot[:, t, w * P:(w + 1) * P], rows[:, t, 0:RC],
                                         start=(w == 1 and fresh is not None and t == a), stop=False,
                                         skip_group_check=True)
                last.then_inc(s.used[h], 1)

            def finish(l, m):
                if l == 1:
                    return
                s = L[l]
                pe.wait_ge(s.xn, m + 1)
                pe.transpose(psT[0][:, 0:P], xn[:, 0, :], ident[:, :]).then_inc(s.xnT, 1)
                pe.wait_ge(s.hT, m + 1)
                pe.matmul(psZ[0][:, 0:F], hT[:, 0, :], wT[:, 3, :], start=True, stop=True)
                pe.matmul(psZ[1][:, 0:F], hT[:, 0, :], wT[:, 4, :], start=True, stop=True).then_inc(s.z, 1)

            def open_banks():
                for k in range(2):
                    pe.matmul(bank[k][:, 0:RC], zeros[:, 0:P], zeros[:, :], start=True, stop=False,
                              skip_group_check=True)

            def begin(l):
                pe.wait_ge(s_one, 1)
                pe.wait_ge(s_iota, 1)
                if l == 1:
                    pe.wait_ge(L[0].evac, NB + 1)
                for h in range(2):
                    pe.sem_inc(L[l].used[h], 1 + h)

            def fast(l):
                s = L[l]
                begin(l)
                open_banks()
                add_rows(l, 0, 0, (1, 0))

                def step(m, k):
                    add_rows(l, m, 1, (k, 1 - k), fresh=m + 1)
                    if is_there(m + 1):
                        add_rows(l, m + 1, 0, (k, 1 - k))
                    finish(l, m)
                in_pairs(pe, step)

            def general(l):
                s = L[l]
                begin(l)
                with pe.Fori(0, NB // 2) as g:
                    pe.wait_ge(s.evac, g * 2 + 1)
                    open_banks()
                    with pe.Fori(0, NB // 2) as i:
                        for k in range(2):
                            for h in range(2):
                                add_rows(l, g * NB + i * 2 + k, h, (0, 1))
                    for k in range(2):
                        finish(l, g * 2 + k)

            for l in range(2):
                either_path(pe, lambda: fast(l), lambda: general(l))

        @block.scalar
        def _(act):
            for j, w in enumerate((w_data, w_ctrl, w_self, w_in, w_out)):
                act.dma_start(w_raw[:, j, :], w).then_inc(s_w, 16)
            for j, b in enumerate((b_data, b_ctrl, b_self)):
                act.dma_start(bias[:, j, :], b.rearrange("(a f) -> a f", a=1).partition_broadcast(P)).then_inc(s_w, 16)
            for j in range(5):
                act.wait_ge(s_wt, j + 1)
                act.activation(wT[:, j, :], (psT + psZ + bank)[j][:, 0:P], ACT.Copy).then_inc(s_wtc, 1)
            g = 0
            for a, to in ((0, dst_f), (1, idx1)):
                for c0 in range(0, CH, 4):
                    act.wait_ge(s_tr, g + 1)
                    n = min(T, (c0 + 4) * P) - c0 * P
                    act.activation(to[:, c0 * P:c0 * P + n], (psT + psZ)[g % 4][:, 0:n], ACT.Copy).then_inc(s_trc, 1)
                    g += 1
            act.wait_ge(s_var, 1)
            act.wait_ge(s_const, 6)
            act.activation(std[:, :], var[:, :], ACT.Sqrt, bias=eps[:, :], scale=1.0 / F).then_inc(s_std, 1)

            def normalise(n, k):
                act.activation(xn[:, k, :], blk(x_sb, n), ACT.Identity, bias=shift[:, bass.ds(n, 1)],
                               scale=rstd[:, bass.ds(n, 1)]).then_inc(s_xn, 1)

            def relu(n, k):
                act.wait_ge(s_xnT, n + 1)
                act.activation(hT[:, k, :], psT[k][:, 0:P], ACT.Relu).then_inc(s_hT, 1)

            def high(n, k):
                if is_there(n + 2):
                    normalise(n + 2, k)
                if is_there(n + 1):
                    relu(n + 1, 1 - k)
                act.wait_ge(s_rfree, n + 1)
                act.wait_ge(s_y, n + 3)
                act.activation(row_out[:, k, :, 0, :], y[:, k, :, :], ACT.Copy).then_inc(s_hi, 1)
            act.wait_ge(s_shift, 1)
            normalise(0, 0)
            normalise(1, 1)
            relu(0, 0)
            in_pairs(act, high)

            def stage(l, seq, n, k):
                s = L[l]
                if not isinstance(seq, int) or seq >= 2:
                    act.wait_ge(s.used[1], seq + 1)
                act.activation(idx_now[:, k, :], (idx0, idx1)[l][:, bass.ds(n * TPB, TPB)], ACT.Copy).then_inc(s.staged, 1)

            def finish(l, m, k):
                s = L[l]
                act.wait_ge(s.agg_free, m + 1)
                act.activation(agg[:, :], bank[k][:, 0:RC], ACT.Copy).then_inc(s.evac, 1)
                if l == 1:
                    return
                act.wait_ge(s.var, m + 1)
                act.activation(std1[:, :], mv1[:, 1:2], ACT.Sqrt, bias=eps[:, :]).then_inc(s.std, 1)
                act.wait_ge(s.xnT, m + 1)
                act.activation(hT[:, 0, :], psT[0][:, 0:P], ACT.Relu).then_inc(s.hT, 1)
                act.wait_ge(s.z, m + 1)
                act.wait_ge(s.rfree, m + 1)
                act.activation(row_out[:, k, 0, 0, :], psZ[0][:, 0:F], ACT.Copy).then_inc(s.hi, 1)
                act.activation(blk(own, m), psZ[1][:, 0:F], ACT.Copy).then_inc(s.own, 1)
                act.wait_ge(s.rest, m + 1)
                act.activation(row_out[:, k, 0, 1, :], rest[:, 0, 0, :], ACT.Copy).then_inc(s.mid, 1)

            def begin(l):
                act.sem_inc(L[l].evac, 1)
                if l == 0:
                    act.wait_ge(s_idx0, 1)

            def fast(l):
                begin(l)
                stage(l, 0, 0, 0)
                stage(l, 1, 1, 1)

                def step(m, k):
                    if is_there(m + 2):
                        stage(l, m + 2, m + 2, k)
                    if is_there(m + 1):
                        act.wait_ge(L[l].used[0], m + 3)
                    else:
                        act.wait_ge(L[l].used[1], NB + 2)
                    finish(l, m, k)
                in_pairs(act, step)

            def general(l):
                begin(l)
                with act.Fori(0, NB // 2) as g:
                    with act.Fori(0, NB // 2) as i:
                        for k in range(2):
                            stage(l, g * NB + i * 2 + k, i * 2 + k, k)
                    act.wait_ge(L[l].used[1], g * NB + NB + 2)
                    for k in range(2):
                        finish(l, g * 2 + k, k)

            for l in range(2):
                either_path(act, lambda: fast(l), lambda: general(l))

        @block.vector
        def _(dve):
            def after(ins, s, n, apart=False):
                ins.then_inc(s, 1)
                if apart:
                    wait_apart(dve, s, n)
                else:
                    dve.wait_ge(s, n)

            dve.wait_ge(s_const, 6)
            dve.tensor_copy(iota_ps[:, 0:W2], iota_i[:, :]).then_inc(s_iota, 1)
            dve.wait_ge(s_edges, EDGE_LOADS)
            dve.tensor_copy(raw[0], raw_i[0]).then_inc(s_float, 1)
            dve.wait_ge(s_x, 32)

            def stat(n, k):
                dve.bn_stats(stats[:, bass.ds(n * 6, 6)], blk(x_sb, n)).then_inc(s_bn, 1)
            in_pairs(dve, stat)
            dve.wait_ge(s_bn, NB)
            dve.tensor_tensor(mean2[:, :], stat_col(1), stat_col(4), op=ALU.add).then_inc(s_mean, 1)
            after(dve.tensor_tensor(var[:, :], stat_col(1), stat_col(4), op=ALU.subtract), s_mean, 2)
            after(dve.tensor_tensor(var[:, :], var[:, :], var[:, :], op=ALU.mult), s_mean, 3)
            after(dve.scalar_tensor_tensor(out=var[:, :], in0=var[:, :], scalar=F / 4.0, in1=stat_col(2),
                                           op0=ALU.mult, op1=ALU.add), s_mean, 4)
            dve.tensor_tensor(var[:, :], var[:, :], stat_col(5), op=ALU.add).then_inc(s_var, 1)
            dve.wait_ge(s_std, 1)
            after(dve.reciprocal(rstd[:, :], std[:, :]), s_rstd, 1)
            dve.scalar_tensor_tensor(out=shift[:, :], in0=mean2[:, :], scalar=-0.5, in1=rstd[:, :],
                                     op0=ALU.mult, op1=ALU.mult).then_inc(s_shift, 1)
            per = -(-CH // 4)
            dve.wait_ge(s_trc, 2 * per)
            for j, c0 in enumerate(range(0, CH, 4)):
                dve.wait_ge(s_tr, 2 * per + j + 1)
                n = min(T, (c0 + 4) * P) - c0 * P
                dve.tensor_scalar(idx0[:, c0 * P:c0 * P + n], (psT + psZ)[(2 * per + j) % 4][:, 0:n], 0.0, float(NPAD),
                                  op0=ALU.not_equal, op1=ALU.mult).then_inc(s_trc, 1)
            dve.wait_ge(s_trc, 3 * per)
            dve.tensor_tensor(idx0[:, :], idx0[:, :], idx1[:, :], op=ALU.add).then_inc(s_idx0, 1)
            far = raw[1][:, 0:T]
            dve.wait_ge(s_bases, 2)
            after(dve.tensor_copy(bases, bases_i), s_far, 1)
            after(dve.tensor_tensor(far, dst_f[:, :], bases, op=ALU.subtract), s_far, 2)
            after(dve.tensor_scalar(far, far, W2 / 2 - 0.5, None, op0=ALU.subtract), s_far, 3)
            after(dve.tensor_tensor(far, far, far, op=ALU.mult), s_far, 4)
            after(dve.tensor_scalar(far, far, float(P * P), None, op0=ALU.is_gt), s_far, 5)
            after(dve.tensor_reduce(missed[:, :], far, axis=mybir.AxisListType.X, op=ALU.add), s_missed, 1)
            dve.memset(rows[:, :, RW:RS], 1.0).then_inc(s_one, 1)
            dve.sem_inc(s_y, 2)

            def biased(n, k):
                dve.wait_ge(s_z, n + 1)
                dve.tensor_tensor(y[:, k, :, :], psZ[k][:, 0:2 * F].rearrange("p (t f) -> p t f", f=F),
                                  bias[:, 0:2, :], op=ALU.add).then_inc(s_yab, 1)
                dve.tensor_tensor(blk(own, n), psZ[k][:, 2 * F:3 * F], bias[:, 2, :], op=ALU.add).then_inc(s_y, 1)

            def middle(n, k):
                if is_there(n + 1):
                    biased(n + 1, 1 - k)
                dve.wait_ge(s_rest, n + 1)
                dve.tensor_copy(row_out[:, k, :, 1, :], rest[:, k, :, :]).then_inc(s_mid, 1)
            biased(0, 0)
            in_pairs(dve, middle)
            dve.wait_ge(s_missum, 1)
            after(dve.tensor_scalar(covered[0:1, 0:1], psM[0:1, 0:1], float(PADS), None, op0=ALU.is_equal), s_covered, 1)

            def make_hot(l, seq, n, moves):
                s = L[l]
                dve.wait_ge(s.based, (seq if moves is None else moves) + 1)
                dve.wait_ge(s.hot[1], seq + 1)
                after(dve.tensor_tensor(rel[:, :], dst_f[:, bass.ds(n * TPB, TPB)], base[:, :], op=ALU.subtract),
                      s.rel, seq + 1)
                if moves is None:
                    dve.tensor_scalar(base[:, :], base[:, :], float(P), None, op0=ALU.add).then_inc(s.based, 1)
                for h, (a, b) in enumerate(HALVES):
                    dve.wait_ge(s.used[h], seq + 1 + h)
                    dve.tensor_tensor(hot[:, a:b, :], iota_ps[:, 0:W2].unsqueeze(1).to_broadcast([P, b - a, W2]),
                                      rel[:, a:b].unsqueeze(2).to_broadcast([P, b - a, W2]),
                                      op=ALU.is_equal).then_inc(s.hot[h], 1)

            def finish(l, m, k):
                s = L[l]
                dve.wait_ge(s.evac, m + 2)
                after(dve.tensor_tensor(low[:, :], agg[:, F:2 * F], agg[:, 2 * F:3 * F], op=ALU.add), s.low, m + 1)
                if l == 1:
                    after(dve.tensor_tensor(tot[:, :], low[:, :], agg[:, 0:F], op=ALU.add), s.tot, m + 1)
                    after(dve.scalar_tensor_tensor(out=tot[:, :], in0=blk(own, m), scalar=agg[:, RW:RC], in1=tot[:, :],
                                                   op0=ALU.mult, op1=ALU.add), s.agg_free, m + 2)
                    dve.wait_ge(s.rfree, m + 1)
                    dve.tensor_tensor(res[:, k, :], tot[:, :], blk(x_sb, m), op=ALU.add).then_inc(s.ready, 1)
                    return
                after(dve.tensor_tensor(tot[:, :], low[:, :], agg[:, 0:F], op=ALU.add), s.agg_free, m + 2)
                after(dve.tensor_tensor(tot[:, :], tot[:, :], blk(own, m), op=ALU.add), s.tot, m + 1)
                after(dve.scalar_tensor_tensor(out=blk(x_sb, m), in0=tot[:, :], scalar=0.0, in1=blk(x_sb, m),
                                               op0=ALU.max, op1=ALU.add), s.x, m + 1, apart=True)
                after(dve.bn_stats(st1[:, :], blk(x_sb, m)), s.bn, m + 1, apart=True)
                after(dve.bn_aggr(mv1[:, :], st1[:, :]), s.var, m + 1)
                dve.wait_ge(s.std, m + 1)
                after(dve.reciprocal(rstd1[:, :], std1[:, :]), s.rstd, m + 1)
                dve.tensor_scalar(xn[:, 0, :], blk(x_sb, m), mv1[:, 0:1], rstd1[:, :],
                                  op0=ALU.subtract, op1=ALU.mult).then_inc(s.xn, 1)
                dve.wait_ge(s.hi, m + 1)
                after(dve.tensor_tensor(rest[:, 0, 0, :], psZ[0][:, 0:F], row_out[:, k, 0, 0, :], op=ALU.subtract),
                      s.rest, m + 1)
                dve.wait_ge(s.mid, m + 1)
                dve.tensor_tensor(row_out[:, k, 0, 2, :], rest[:, 0, 0, :], row_out[:, k, 0, 1, :],
                                  op=ALU.subtract).then_inc(s.ready, 1)

            def fast(l):
                s = L[l]
                dve.sem_inc(s.agg_free, 1)
                dve.sem_inc(s.hot[1], 1)
                dve.tensor_copy(base[:, :], base_i[:, :]).then_inc(s.based, 1)
                make_hot(l, 0, 0, None)

                def step(m, k):
                    if is_there(m + 1):
                        make_hot(l, m + 1, m + 1, None)
                    finish(l, m, k)
                in_pairs(dve, step)

            def general(l):
                s = L[l]
                dve.sem_inc(s.agg_free, 1)
                dve.sem_inc(s.hot[1], 1)
                dve.memset(base[:, :], 0.0).then_inc(s.based, 1)
                with dve.Fori(0, NB // 2) as g:
                    with dve.Fori(0, NB // 2) as i:
                        for k in range(2):
                            make_hot(l, g * NB + i * 2 + k, i * 2 + k, g)
                    dve.tensor_scalar(base[:, :], base[:, :], float(W2), None, op0=ALU.add).then_inc(s.based, 1)
                    for k in range(2):
                        finish(l, g * 2 + k, k)

            for l in range(2):
                if l == 1:
                    dve.wait_ge(L[0].own, NB)
                either_path(dve, lambda: fast(l), lambda: general(l))


_INS = ["x", "src", "dst", "edge_type_2", "L0_gnn_W_data", "L0_gnn_b_data", "L0_gnn_W_control", "L0_gnn_b_control",
        "L0_gnn_W_self", "L0_gnn_b_self", "L1_gnn_W_in", "L1_gnn_W_out"]


def kernel(**inputs):
    import numpy as _np
    import concourse.bacc as _bacc
    from concourse import mybir as _mybir
    from concourse.bass_utils import run_bass_kernel_spmd as _run

    nc = _bacc.Bacc("TRN2", target_bir_lowering=False, num_devices=1)
    arrays, args = {}, []
    for name in _INS:
        a = _np.ascontiguousarray(inputs[name])
        arrays[f"in_{name}_dram"] = a
        args.append(nc.dram_tensor(f"in_{name}_dram", a.shape, _mybir.dt.from_np(a.dtype), kind="ExternalInput").ap())
    out = nc.dram_tensor("out_dram", inputs["x"].shape, _mybir.dt.float32, kind="ExternalOutput").ap()
    gnn_kernel(nc, *args, out)
    r = _run(nc, [arrays], core_ids=[0])
    return r.results[0]["out_dram"]
```

```python
import concourse.bass as bass
from concourse import mybir
from contextlib import ExitStack

P = 128



def gnn_kernel(nc, x, src, dst, etype, w_data, b_data, w_ctrl, b_ctrl, w_self, b_self, w_in, w_out, out):
    fp32, bf16, i32 = mybir.dt.float32, mybir.dt.bfloat16, mybir.dt.int32
    ALU, ACT = mybir.AluOpType, mybir.ActivationFunctionType
    EPS = 1e-5

    N, F = x.shape
    E = src.shape[0]
    assert F == P
    NB = -(-N // P)
    LAST = N - (NB - 1) * P
    TPB = -(-E // N)
    T = NB * TPB
    assert NB % 2 == 0 and NB >= 4 and T * P >= E
    NPAD = NB * P
    HALVES = ((0, (TPB + 1) // 2), ((TPB + 1) // 2, TPB))
    TA = HALVES[0][1]
    PARTS = 3
    RW = PARTS * F
    RC = RW + 1
    RS = RC + 1
    W2 = 2 * P

    CH = -(-T // P)
    FULL = E // P
    REM = E - FULL * P
    FCH = FULL // P
    XTRA = FULL - FCH * P
    PAD_NODE = NPAD
    PIECES = 16 * ((FCH > 0) + (XTRA > 0) + (REM > 0))
    REAL = -(-E // P) - (NB - 1) * TPB
    assert TA < REAL <= TPB
    XCH = min(7, NB // 2)
    XB = [NB * c // XCH for c in range(XCH + 1)]

    table0 = nc.dram_tensor("table0", (2 * NPAD, RW), bf16, kind="Internal").ap()
    table1 = nc.dram_tensor("table1", (NPAD, RW), bf16, kind="Internal").ap()
    table0_blocks = table0.rearrange("(t q) c -> q t c", t=2)

    ctx = ExitStack()
    with ctx:
        def sb(name, shape, dt):
            return ctx.enter_context(nc.sbuf_tensor(name, shape, dt))

        def pb(name, shape, dt=fp32):
            return ctx.enter_context(nc.psum_tensor(name, shape, dt))

        def sem(name):
            return ctx.enter_context(nc.semaphore(name))

        x_sb = sb("x_sb", [P, NB * F], fp32)
        own = sb("own", [P, NB * F], fp32)
        idx0 = sb("idx0", [P, T], fp32)
        idx1 = sb("idx1", [P, T], fp32)
        dst_f = sb("dst_f", [P, T], fp32)
        row_words = TPB * RS // 2 + (TPB * RS) % 2
        hot_words = TPB * W2 // 2
        arena_words = max(row_words + hot_words, 3 * CH * P)
        arena = sb("arena", [P, arena_words], fp32)
        rows = arena[:, 0:row_words].bitcast(bf16)[:, 0:TPB * RS].rearrange("p (t c) -> p t c", c=RS)
        hot = arena[:, row_words:row_words + hot_words].bitcast(bf16).rearrange("p (t c) -> p t c", c=W2)
        raw = [arena[:, a * CH * P:(a + 1) * CH * P] for a in range(3)]
        raw_i = [r.bitcast(i32) for r in raw]

        idx_now = sb("idx_now", [P, 2, TPB], i32)
        base = sb("base", [P, TPB], fp32)
        base_0 = sb("base_0", [P, TPB], fp32)
        rel = sb("rel", [P, TPB], fp32)
        bases = own[:, 0:CH * P]
        ident = sb("ident", [P, P], fp32)
        ones = sb("ones", [P, 1], fp32)
        zeros = sb("zeros", [P, RC], bf16)
        eps = sb("eps", [P, 1], fp32)
        iota = sb("iota", [P, W2], fp32)
        w_raw = sb("w_raw", [P, 5, F], fp32)
        wT = sb("wT", [P, 5, F], fp32)
        bias = sb("bias", [P, 3, F], fp32)
        stats = sb("stats", [P, NB * 6], fp32)
        mean2 = sb("mean2", [P, NB], fp32)
        var = sb("var", [P, NB], fp32)
        std = sb("std", [P, NB], fp32)
        rstd = sb("rstd", [P, NB], fp32)
        shift = sb("shift", [P, NB], fp32)
        root = sb("root", [P, 1], fp32)

        def stat_col(c):
            return stats[:, :].rearrange("p (n c) -> p n c", c=6)[:, :, c]
        tmax = sb("tmax", [P, CH], fp32)
        tmin = sb("tmin", [P, CH], fp32)
        missed = sb("missed", [P, 1], fp32)
        covered = sb("covered", [1, 1], i32)
        xn = sb("xn", [P, 2, F], fp32)
        hT = sb("hT", [P, 2, P], fp32)
        y = sb("y", [P, 2, 2, F], fp32)
        rest = sb("rest", [P, 2, 2, F], fp32)
        row_out = sb("row_out", [P, 4, 2, PARTS, F], bf16)
        agg = sb("agg", [P, RC], fp32)
        low = sb("low", [P, F], fp32)
        tot = sb("tot", [P, F], fp32)
        res = sb("res", [P, 2, F], fp32)
        xn_own = y[:, 0, 0, :]
        hT_own = hT[:, 1, :]
        own0 = y[:, 0, 1, :]
        st1 = sb("st1", [P, 6], fp32)
        mv1 = sb("mv1", [P, 2], fp32)
        std1 = sb("std1", [P, 1], fp32)
        rstd1 = sb("rstd1", [P, 1], fp32)

        bank = [pb(f"bank{k}", [P, 512]) for k in range(2)]
        psT = [pb(f"psT{k}", [P, 512]) for k in range(2)]
        psZ = [pb(f"psZ{k}", [P, 512]) for k in range(2)]
        iota_ps = pb("iota_ps", [P, 512])
        psM = pb("psM", [P, 512])

        def blk(t, n):
            return t[:, bass.ds(n * F, F)]

        s_edges = [sem(f"s_edges_{a}") for a in ("dst", "type", "src")]
        s_w = sem("s_w")
        s_x = [sem(f"s_x{c}") for c in range(XCH)]
        s_pads = sem("s_pads")
        s_const = sem("s_const")
        s_ident = sem("s_ident")
        s_float = [sem(f"s_float_{a}") for a in ("dst", "idx0", "src")]
        s_tr = sem("s_tr")
        s_trc = sem("s_trc")
        s_wt = sem("s_wt")
        s_wtc = sem("s_wtc")
        s_root = sem("s_root")
        s_iota = sem("s_iota")
        s_bn = sem("s_bn")
        s_rstd = sem("s_rstd")
        s_typed = sem("s_typed")
        s_extent = sem("s_extent")
        s_centre = sem("s_centre")
        s_far = sem("s_far")
        s_bases = sem("s_bases")
        s_missed = sem("s_missed")
        s_missum = sem("s_missum")
        s_covered = sem("s_covered")
        s_var = sem("s_var")
        s_mean = sem("s_mean")
        s_std = sem("s_std")
        s_shift = sem("s_shift")
        s_xn = sem("s_xn")
        s_xnT = sem("s_xnT")
        s_hT = sem("s_hT")
        s_z = sem("s_z")
        s_y = sem("s_y")
        s_hi = sem("s_hi")
        s_rest = sem("s_rest")
        s_mid = sem("s_mid")
        s_low = sem("s_low")
        s_st0 = [sem(f"s_st0{k}") for k in range(4)]
        s_st1 = [sem(f"s_st1{k}") for k in range(2)]
        s_out = [sem(f"s_out{k}") for k in range(2)]
        s_one = sem("s_one")

        class Layer:
            pass

        L = []
        for l in range(2):
            s = Layer()
            s.staged = sem(f"l{l}_staged")
            s.gathered = [sem(f"l{l}_gathered{h}") for h in "AB"]
            s.based = sem(f"l{l}_based")
            s.rel = sem(f"l{l}_rel")
            s.hot = [sem(f"l{l}_hot{h}") for h in "AB"]
            s.used = [sem(f"l{l}_used{h}") for h in "AB"]
            s.evac = sem(f"l{l}_evac")
            s.agg_free = sem(f"l{l}_agg_free")
            s.own_xn = sem(f"l{l}_own_xn")
            s.own_xnT = sem(f"l{l}_own_xnT")
            s.own_hT = sem(f"l{l}_own_hT")
            s.own_z = sem(f"l{l}_own_z")
            s.own_b = sem(f"l{l}_own_b")
            s.low = sem(f"l{l}_low")
            s.tot = sem(f"l{l}_tot")
            s.x = sem(f"l{l}_x")
            s.bn = sem(f"l{l}_bn")
            s.var = sem(f"l{l}_var")
            s.std = sem(f"l{l}_std")
            s.rstd = sem(f"l{l}_rstd")
            s.xn = sem(f"l{l}_xn")
            s.xnT = sem(f"l{l}_xnT")
            s.hT = sem(f"l{l}_hT")
            s.z = sem(f"l{l}_z")
            s.hi = sem(f"l{l}_hi")
            s.rest = sem(f"l{l}_rest")
            s.mid = sem(f"l{l}_mid")
            s.ready = sem(f"l{l}_ready")
            s.rfree = sem(f"l{l}_rfree")
            s.own = sem(f"l{l}_own")
            L.append(s)

        s_apart = {nc.gpsimd.engine: sem("s_apart_pool"), nc.vector.engine: sem("s_apart_dve")}

        block = ctx.enter_context(nc.Block())

        def in_pairs(eng, step):
            with eng.Fori(0, NB // 2 - 1) as i:
                for k in range(2):
                    step(i * 2 + k, k)
            for k in range(2):
                step(NB - 2 + k, k)

        def in_fours(eng, step):
            fours = (NB - 4) // 4
            if fours < 2:
                fours = 1
            for j in range(4):
                step(j, 0, j)
            if fours > 1:
                with eng.Fori(1, fours) as i:
                    for j in range(4):
                        step(i * 4 + j, i, j)
            for n in range(4 * fours, NB):
                step(n, n // 4, n % 4)

        def is_there(n):
            return not isinstance(n, int) or n < NB

        def wait_apart(eng, semaphore, n):
            eng.wait_ge(semaphore, n)
            eng.sem_inc(s_apart[eng.engine], 1)

        def either_path(eng, fast, general):
            eng.wait_ge(s_covered, 1)
            with eng.If(eng.value_load(covered[0:1, 0:1], min_val=0, max_val=1) == 1):
                fast()
            with eng.Else():
                general()

        @block.sync
        def _(sp):
            for l in range(2):
                sp.sem_inc(L[l].rfree, 2)
            sp.wait_ge(s_pads, 4)
            for a, lst in enumerate((dst, etype, src)):
                if FCH:
                    sp.dma_start(raw_i[a][:, 0:FCH * P].rearrange("p (c e) -> p c e", e=P),
                                 lst[0:FCH * P * P].rearrange("(c p e) -> p c e", p=P, e=P)).then_inc(s_edges[a], 16)
                if XTRA:
                    sp.dma_start(raw_i[a][0:XTRA, FCH * P:FCH * P + P],
                                 lst[FCH * P * P:FULL * P].rearrange("(p e) -> p e", e=P)).then_inc(s_edges[a], 16)
                if REM:
                    sp.dma_start(raw_i[a][XTRA:XTRA + 1, FCH * P:FCH * P + REM],
                                 lst[FULL * P:E].rearrange("(p e) -> p e", p=1)).then_inc(s_edges[a], 16)
            for c in range(XCH):
                n0, n1 = XB[c], min(XB[c + 1], NB - 1)
                sp.dma_start(x_sb[:, n0 * F:n1 * F].rearrange("p (n f) -> p n f", f=F),
                             x[n0 * P:n1 * P, :].rearrange("(n p) f -> p n f", p=P)).then_inc(s_x[c], 16)
            sp.dma_start(x_sb[0:LAST, (NB - 1) * F:NB * F], x[(NB - 1) * P:N, :]).then_inc(s_x[XCH - 1], 16)

            def store0(n, i, j):
                sp.wait_ge(s_low, n + 1)
                sp.dma_start(table0_blocks[bass.ds(n * P, P), :, :],
                             row_out[:, j, :, :, :].rearrange("p t a f -> p t (a f)")).then_inc(s_st0[j], 16)
            in_fours(sp, store0)

            def store(l, m, k):
                s = L[l]
                sp.wait_ge(s.ready, m + 1)
                done = (s_st1, s_out)[l]
                if l == 0:
                    sp.dma_start(table1[bass.ds(m * P, P), :],
                                 row_out[:, k, 0, :, :].rearrange("p a f -> p (a f)")).then_inc(done[k], 16)
                elif isinstance(m, int) and m == NB - 1:
                    sp.dma_start(out[m * P:N, :], res[0:LAST, k, :]).then_inc(done[k], 16)
                else:
                    sp.dma_start(out[bass.ds(m * P, P), :], res[:, k, :]).then_inc(done[k], 16)
                if k == 1:
                    for j in range(2):
                        sp.wait_ge(done[j], (m - 1) * 8 + 16)
                        sp.sem_inc(s.rfree, 1)

            for l in range(2):
                in_pairs(sp, lambda m, k: store(l, m, k))
            for k in range(2):
                sp.wait_ge(s_out[k], 16 * (NB // 2))

        @block.gpsimd
        def _(pool):
            for a, v in enumerate((PAD_NODE, 0, 0)):
                pool.memset(raw_i[a][:, FCH * P:CH * P], v).then_inc(s_pads, 1)
            pool.memset(x_sb[:, (NB - 1) * F:NB * F], 0.0).then_inc(s_pads, 1)
            pool.memset(ident[:, :], 0.0).then_inc(s_ident, 1)
            pool.memset(ones[:, :], 1.0).then_inc(s_const, 1)
            pool.memset(zeros[:, :], 0.0).then_inc(s_const, 1)
            pool.memset(eps[:, :], EPS).then_inc(s_const, 1)
            pool.wait_ge(s_ident, 1)
            pool.affine_select(out=ident[:, :], in_=ident[:, :], compare_op=ALU.not_equal, fill=1.0,
                               base=0, pattern=[[-1, P]], channel_multiplier=1).then_inc(s_ident, 1)
            pool.iota(iota[:, :], [[1, W2]], base=0, channel_multiplier=0,
                      allow_small_or_imprecise_dtypes=True).then_inc(s_const, 1)
            for h, (a, b) in enumerate(HALVES):
                pool.iota(base_0[:, a:b], [[0, b - a]], base=(h - 1) * P, channel_multiplier=0,
                          allow_small_or_imprecise_dtypes=True).then_inc(s_const, 1)
                pool.iota(bases[:, 0:T].rearrange("p (n t) -> p n t", t=TPB)[:, :, a:b], [[P, NB], [0, b - a]],
                          base=(h - 1) * P, channel_multiplier=0,
                          allow_small_or_imprecise_dtypes=True).then_inc(s_bases, 1)
            pool.memset(bases[:, T:CH * P], float((NB - 1) * P)).then_inc(s_bases, 1)

            def split(n, i, j):
                pool.wait_ge(s_hi, n + 1)
                pool.tensor_tensor(rest[:, j % 2, :, :], y[:, j % 2, :, :], row_out[:, j, :, 0, :],
                                   op=ALU.subtract).then_inc(s_rest, 1)
            in_fours(pool, split)
            for j in range(4):
                pool.wait_ge(s_st0[j], 16 * len(range(j, NB, 4)))

            def gather(l, seq, k):
                s = L[l]
                wait_apart(pool, s.staged, seq + 1)
                for h, (a, b) in enumerate(HALVES):
                    if isinstance(seq, int) and seq == NB - 1:
                        b = min(b, REAL)
                    wait_apart(pool, s.used[h], seq + 1 + h)
                    for t in range(a, b):
                        pool.indirect_dma_start(
                            out=rows[:, t, 0:RW], out_offset=None, in_=(table0, table1)[l],
                            in_offset=bass.IndirectOffsetOnAxis(ap=idx_now[:, k, t:t + 1], axis=0),
                            compute_op=ALU.bypass).then_inc(s.gathered[h], 16)

            def gather_general(l):
                with pool.Fori(0, NB // 2) as g:
                    with pool.Fori(0, NB // 2) as i:
                        for k in range(2):
                            gather(l, g * NB + i * 2 + k, k)

            for l in range(2):
                if l == 1:
                    for k in range(2):
                        pool.wait_ge(s_st1[k], 16 * (NB // 2))
                either_path(pool, lambda: in_pairs(pool, lambda n, k: gather(l, n, k)), lambda: gather_general(l))

        @block.tensor
        def _(pe):
            pe.wait_ge(s_ident, 2)
            pe.wait_ge(s_w, 16 * 8)
            for j in range(5):
                pe.transpose((psT + psZ + bank)[j][:, 0:P], w_raw[:, j, :], ident[:, :]).then_inc(s_wt, 1)
            pe.wait_ge(s_wtc, 5)
            g = 0
            for a, made in ((0, s_float[0]), (2, s_float[2]), (1, s_float[1])):
                pe.wait_ge(made, 1)
                for c0 in range(0, CH, 4):
                    if g >= 4:
                        pe.wait_ge(s_trc, g - 3)
                    for c in range(c0, min(c0 + 4, CH)):
                        last = pe.transpose((psT + psZ)[g % 4][:, (c - c0) * P:(c - c0 + 1) * P],
                                            raw[a][:, c * P:(c + 1) * P], ident[:, :])
                    last.then_inc(s_tr, 1)
                    g += 1
            pe.wait_ge(s_bases, 3)
            pe.wait_ge(s_const, 6)
            for c in range(CH):
                last = pe.matmul(psM[:, c:c + 1], bases[0:1, c * P:(c + 1) * P], ones[0:1, 0:1],
                                 start=(c == 0), stop=(c == CH - 1), skip_group_check=True)
            last.then_inc(s_centre, 1)
            pe.wait_ge(s_trc, g)

            def turn(n, k):
                pe.wait_ge(s_xn, n + 1)
                pe.transpose(psT[k][:, 0:P], xn[:, k, :], ident[:, :]).then_inc(s_xnT, 1)

            def multiply(n, i, j):
                k = j % 2
                pe.wait_ge(s_hT, n + 1)
                pe.wait_ge(s_y, n + 1)
                pe.matmul(psZ[k][:, 0:2 * F], hT[:, k, :], wT[:, 0:2, :].rearrange("p j f -> p (j f)"),
                          start=True, stop=True).then_inc(s_z, 1)
                if is_there(n + 2):
                    turn(n + 2, k)
            turn(0, 0)
            turn(1, 1)
            in_fours(pe, multiply)
            pe.wait_ge(s_missed, 1)
            pe.matmul(psM[0:1, 0:1], missed[:, :], ones[:, :], start=True, stop=True).then_inc(s_missum, 1)

            def add_rows(l, seq, h, to, fresh=None):
                s = L[l]
                pe.wait_ge(s.hot[h], seq + 2 if h else seq + 1)
                if fresh is not None:
                    pe.wait_ge(s.evac, fresh)
                a, b = HALVES[h]
                before = seq * (16 * (b - a))
                if fresh is not None and isinstance(seq, int) and seq == NB - 1:
                    b = REAL
                pe.wait_ge(s.gathered[h], before + 16 * (b - a))
                for t in range(a, b):
                    for w in range(2):
                        last = pe.matmul(bank[to[w]][:, 0:RC], hot[:, t, w * P:(w + 1) * P], rows[:, t, 0:RC],
                                         start=(w == 1 and fresh is not None and t == a), stop=False,
                                         skip_group_check=True)
                last.then_inc(s.used[h], 1)

            def own_turn(l, m):
                if l == 0:
                    pe.wait_ge(L[l].own_xn, m + 1)
                    pe.transpose(psM[:, 0:P], xn_own, ident[:, :]).then_inc(L[l].own_xnT, 1)

            def own_multiply(l, m):
                if l == 0:
                    pe.wait_ge(L[l].own_hT, m + 1)
                    pe.matmul(psM[:, 0:F], hT_own, wT[:, 2, :], start=True, stop=True).then_inc(L[l].own_z, 1)

            def finish(l, m):
                if l == 1:
                    return
                s = L[l]
                pe.wait_ge(s.xn, m + 1)
                pe.transpose(psT[0][:, 0:P], xn[:, 0, :], ident[:, :]).then_inc(s.xnT, 1)
                pe.wait_ge(s.hT, m + 1)
                pe.matmul(psZ[0][:, 0:F], hT[:, 0, :], wT[:, 3, :], start=True, stop=True)
                pe.matmul(psZ[1][:, 0:F], hT[:, 0, :], wT[:, 4, :], start=True, stop=True).then_inc(s.z, 1)

            def open_banks():
                for k in range(2):
                    pe.matmul(bank[k][:, 0:RC], zeros[:, 0:P], zeros[:, :], start=True, stop=False,
                              skip_group_check=True)

            def begin(l):
                pe.wait_ge(s_one, 1)
                pe.wait_ge(s_iota, 1)
                if l == 1:
                    pe.wait_ge(L[0].evac, NB + 1)
                for h in range(2):
                    pe.sem_inc(L[l].used[h], 1 + h)

            def fast(l):
                s = L[l]
                begin(l)
                open_banks()
                add_rows(l, 0, 0, (1, 0))

                def step(m, k):
                    add_rows(l, m, 1, (k, 1 - k), fresh=m + 1)
                    own_turn(l, m)
                    if is_there(m + 1):
                        add_rows(l, m + 1, 0, (k, 1 - k))
                    own_multiply(l, m)
                    finish(l, m)
                in_pairs(pe, step)

            def general(l):
                s = L[l]
                begin(l)
                with pe.Fori(0, NB // 2) as g:
                    pe.wait_ge(s.evac, g * 2 + 1)
                    open_banks()
                    with pe.Fori(0, NB // 2) as i:
                        for k in range(2):
                            for h in range(2):
                                add_rows(l, g * NB + i * 2 + k, h, (0, 1))
                    for k in range(2):
                        own_turn(l, g * 2 + k)
                        own_multiply(l, g * 2 + k)
                        finish(l, g * 2 + k)

            for l in range(2):
                either_path(pe, lambda: fast(l), lambda: general(l))

        @block.scalar
        def _(act):
            for j, w in enumerate((w_data, w_ctrl, w_self, w_in, w_out)):
                act.dma_start(w_raw[:, j, :], w).then_inc(s_w, 16)
            for j, b in enumerate((b_data, b_ctrl, b_self)):
                act.dma_start(bias[:, j, :], b.rearrange("(a f) -> a f", a=1).partition_broadcast(P)).then_inc(s_w, 16)
            act.wait_ge(s_const, 6)
            act.activation(root[:, :], eps[:, :], ACT.Sqrt).then_inc(s_root, 1)
            for j in range(5):
                act.wait_ge(s_wt, j + 1)
                act.activation(wT[:, j, :], (psT + psZ + bank)[j][:, 0:P], ACT.Copy).then_inc(s_wtc, 1)
            act.wait_ge(s_edges[2], PIECES)
            act.activation(raw[2], raw_i[2], ACT.Copy).then_inc(s_float[2], 1)
            g = 0
            for to in (dst_f, idx1, idx0):
                for c0 in range(0, CH, 4):
                    act.wait_ge(s_tr, g + 1)
                    n = min(T, (c0 + 4) * P) - c0 * P
                    act.activation(to[:, c0 * P:c0 * P + n], (psT + psZ)[g % 4][:, 0:n], ACT.Copy).then_inc(s_trc, 1)
                    g += 1
            act.wait_ge(s_const, 6)
            act.wait_ge(s_var, 1)
            act.activation(std[:, :], var[:, :], ACT.Sqrt, bias=eps[:, :], scale=1.0 / F).then_inc(s_std, 1)

            def relu(n, k):
                act.wait_ge(s_xnT, n + 1)
                act.activation(hT[:, k, :], psT[k][:, 0:P], ACT.Relu).then_inc(s_hT, 1)

            def high(n, four, slot):
                if not isinstance(four, int) or four > 0:
                    act.wait_ge(s_st0[slot], four * 16)
                act.wait_ge(s_y, n + 3)
                act.activation(row_out[:, slot, :, 0, :], y[:, slot % 2, :, :], ACT.Copy).then_inc(s_hi, 1)

            def convert(n, i, j):
                if is_there(n + 3):
                    relu(n + 3, (j + 3) % 2)
                act.wait_ge(s_rest, n + 1)
                act.activation(row_out[:, j, :, 1, :], rest[:, j % 2, :, :], ACT.Copy).then_inc(s_mid, 1)
                if is_there(n + 1):
                    high(n + 1, i + (j + 1) // 4, (j + 1) % 4)
            relu(0, 0)
            relu(1, 1)
            relu(2, 0)
            high(0, 0, 0)
            in_fours(act, convert)

            def stage(l, seq, n, k):
                s = L[l]
                if not isinstance(seq, int) or seq >= 2:
                    act.wait_ge(s.used[1], seq + 1)
                act.activation(idx_now[:, k, :], (idx0, idx1)[l][:, bass.ds(n * TPB, TPB)], ACT.Copy).then_inc(s.staged, 1)

            def own_relu(l, m):
                if l == 0:
                    act.wait_ge(L[l].own_xnT, m + 1)
                    act.activation(hT_own, psM[:, 0:P], ACT.Relu).then_inc(L[l].own_hT, 1)

            def finish(l, m, k):
                s = L[l]
                act.wait_ge(s.agg_free, m + 1)
                act.activation(agg[:, :], bank[k][:, 0:RC], ACT.Copy).then_inc(s.evac, 1)
                if l == 1:
                    return
                act.wait_ge(s.var, m + 1)
                act.activation(std1[:, :], mv1[:, 1:2], ACT.Sqrt, bias=eps[:, :]).then_inc(s.std, 1)
                act.wait_ge(s.xnT, m + 1)
                act.activation(hT[:, 0, :], psT[0][:, 0:P], ACT.Relu).then_inc(s.hT, 1)
                act.wait_ge(s.z, m + 1)
                act.wait_ge(s.rfree, m + 1)
                act.activation(row_out[:, k, 0, 0, :], psZ[0][:, 0:F], ACT.Copy).then_inc(s.hi, 1)
                act.activation(blk(own, m), psZ[1][:, 0:F], ACT.Copy).then_inc(s.own, 1)
                act.wait_ge(s.rest, m + 1)
                act.activation(row_out[:, k, 0, 1, :], rest[:, 0, 0, :], ACT.Copy).then_inc(s.mid, 1)

            def begin(l):
                act.sem_inc(L[l].evac, 1)

            def fast(l):
                begin(l)
                stage(l, 0, 0, 0)
                stage(l, 1, 1, 1)

                def step(m, k):
                    if is_there(m + 2):
                        stage(l, m + 2, m + 2, k)
                    own_relu(l, m)
                    if is_there(m + 1):
                        act.wait_ge(L[l].used[0], m + 3)
                    else:
                        act.wait_ge(L[l].used[1], NB + 2)
                    finish(l, m, k)
                in_pairs(act, step)

            def general(l):
                begin(l)
                with act.Fori(0, NB // 2) as g:
                    with act.Fori(0, NB // 2) as i:
                        for k in range(2):
                            stage(l, g * NB + i * 2 + k, i * 2 + k, k)
                    act.wait_ge(L[l].used[1], g * NB + NB + 2)
                    for k in range(2):
                        own_relu(l, g * 2 + k)
                        finish(l, g * 2 + k, k)

            for l in range(2):
                either_path(act, lambda: fast(l), lambda: general(l))

        @block.vector
        def _(dve):
            def after(ins, s, n, apart=False):
                ins.then_inc(s, 1)
                if apart:
                    wait_apart(dve, s, n)
                else:
                    dve.wait_ge(s, n)

            dve.wait_ge(s_const, 6)
            dve.tensor_copy(iota_ps[:, 0:W2], iota[:, :]).then_inc(s_iota, 1)
            dve.wait_ge(s_edges[0], PIECES)
            after(dve.tensor_copy(raw[0], raw_i[0]), s_float[0], 1)
            dst_tiles = raw[0].rearrange("p (c e) -> p c e", e=P)
            dve.tensor_reduce(tmax[:, :], dst_tiles, axis=mybir.AxisListType.X, op=ALU.max).then_inc(s_extent, 1)
            dve.tensor_reduce(tmin[:, :], dst_tiles, axis=mybir.AxisListType.X, op=ALU.min).then_inc(s_extent, 1)
            dve.wait_ge(s_edges[1], PIECES)
            after(dve.tensor_scalar(raw[1], raw_i[1], 0.0, float(NPAD), op0=ALU.not_equal, op1=ALU.mult), s_typed, 1)
            dve.wait_ge(s_float[2], 1)
            dve.tensor_tensor(raw[1], raw[1], raw[2], op=ALU.add).then_inc(s_float[1], 1)

            def stat(n):
                dve.bn_stats(stats[:, bass.ds(n * 6, 6)], blk(x_sb, n)).then_inc(s_bn, 1)
            for c in range(XCH):
                dve.wait_ge(s_x[c], 32 if c == XCH - 1 else 16)
                some = (XB[c + 1] - XB[c]) // 2
                with dve.Fori(0, 2) as i:
                    for n in range(some):
                        stat(i * some + (XB[c] + n))
                for n in range(XB[c] + 2 * some, XB[c + 1]):
                    stat(n)
            dve.wait_ge(s_bn, NB)
            dve.tensor_tensor(mean2[:, :], stat_col(1), stat_col(4), op=ALU.add).then_inc(s_mean, 1)
            after(dve.tensor_tensor(var[:, :], stat_col(1), stat_col(4), op=ALU.subtract), s_mean, 2)
            after(dve.tensor_tensor(var[:, :], var[:, :], var[:, :], op=ALU.mult), s_mean, 3)
            after(dve.scalar_tensor_tensor(out=var[:, :], in0=var[:, :], scalar=F / 4.0, in1=stat_col(2),
                                           op0=ALU.mult, op1=ALU.add), s_mean, 4)
            dve.tensor_tensor(var[:, :], var[:, :], stat_col(5), op=ALU.add).then_inc(s_var, 1)
            dve.wait_ge(s_std, 1)
            after(dve.reciprocal(rstd[:, :], std[:, :]), s_rstd, 1)
            dve.scalar_tensor_tensor(out=shift[:, :], in0=mean2[:, :], scalar=-0.5, in1=rstd[:, :],
                                     op0=ALU.mult, op1=ALU.mult).then_inc(s_shift, 1)
            dve.wait_ge(s_extent, 2)
            dve.wait_ge(s_centre, 1)
            dve.tensor_tensor(tmax[:, :], tmax[:, :], psM[:, 0:CH], op=ALU.subtract).then_inc(s_far, 1)
            after(dve.tensor_tensor(tmin[:, :], tmin[:, :], psM[:, 0:CH], op=ALU.subtract), s_far, 2)
            after(dve.tensor_scalar(tmax[:, :], tmax[:, :], W2 - 0.5, None, op0=ALU.is_gt), s_far, 3)
            after(dve.scalar_tensor_tensor(out=tmin[:, :], in0=tmin[:, :], scalar=-0.5, in1=tmax[:, :],
                                           op0=ALU.is_lt, op1=ALU.add), s_far, 4)
            dve.tensor_reduce(missed[:, :], tmin[:, :], axis=mybir.AxisListType.X, op=ALU.add).then_inc(s_missed, 1)
            dve.wait_ge(s_trc, 3 * -(-CH // 4))
            dve.memset(rows[:, :, RW:RS], 1.0).then_inc(s_one, 1)
            dve.sem_inc(s_y, 2)

            def normalise(to, n):
                return dve.tensor_scalar(to, blk(x_sb, n), rstd[:, bass.ds(n, 1)], shift[:, bass.ds(n, 1)],
                                         op0=ALU.mult, op1=ALU.add)

            def biased(n, k):
                dve.wait_ge(s_z, n + 1)
                dve.tensor_tensor(y[:, k, :, :], psZ[k][:, 0:2 * F].rearrange("p (t f) -> p t f", f=F),
                                  bias[:, 0:2, :], op=ALU.add).then_inc(s_y, 1)

            def lowest(n, i, j):
                if is_there(n + 1):
                    biased(n + 1, (j + 1) % 2)
                if is_there(n + 4):
                    normalise(xn[:, j % 2, :], n + 4).then_inc(s_xn, 1)
                dve.wait_ge(s_mid, n + 1)
                dve.tensor_tensor(row_out[:, j, :, 2, :], rest[:, j % 2, :, :], row_out[:, j, :, 1, :],
                                  op=ALU.subtract).then_inc(s_low, 1)
            dve.wait_ge(s_shift, 1)
            for n in range(4):
                if n >= 2:
                    dve.wait_ge(s_xnT, n - 1)
                normalise(xn[:, n % 2, :], n).then_inc(s_xn, 1)
            biased(0, 0)
            in_fours(dve, lowest)
            dve.wait_ge(s_missum, 1)
            after(dve.tensor_scalar(covered[0:1, 0:1], psM[0:1, 0:1], 0.0, None, op0=ALU.is_equal), s_covered, 1)

            def make_hot(l, seq, n, moves):
                s = L[l]
                dve.wait_ge(s.based, (seq if moves is None else moves) + 1)
                dve.wait_ge(s.hot[1], seq + 1)
                after(dve.tensor_tensor(rel[:, :], dst_f[:, bass.ds(n * TPB, TPB)], base[:, :], op=ALU.subtract),
                      s.rel, seq + 1)
                if moves is None:
                    dve.tensor_scalar(base[:, :], base[:, :], float(P), None, op0=ALU.add).then_inc(s.based, 1)
                for h, (a, b) in enumerate(HALVES):
                    dve.wait_ge(s.used[h], seq + 1 + h)
                    dve.tensor_tensor(hot[:, a:b, :], iota_ps[:, 0:W2].unsqueeze(1).to_broadcast([P, b - a, W2]),
                                      rel[:, a:b].unsqueeze(2).to_broadcast([P, b - a, W2]),
                                      op=ALU.is_equal).then_inc(s.hot[h], 1)

            def own_normalise(l, m):
                if l == 0:
                    normalise(xn_own, m).then_inc(L[l].own_xn, 1)

            def finish(l, m, k):
                s = L[l]
                dve.wait_ge(s.evac, m + 2)
                after(dve.tensor_tensor(low[:, :], agg[:, F:2 * F], agg[:, 2 * F:3 * F], op=ALU.add), s.low, m + 1)
                if l == 1:
                    after(dve.tensor_tensor(tot[:, :], low[:, :], agg[:, 0:F], op=ALU.add), s.tot, m + 1)
                    after(dve.scalar_tensor_tensor(out=tot[:, :], in0=blk(own, m), scalar=agg[:, RW:RC], in1=tot[:, :],
                                                   op0=ALU.mult, op1=ALU.add), s.agg_free, m + 2)
                    dve.wait_ge(s.rfree, m + 1)
                    dve.tensor_tensor(res[:, k, :], tot[:, :], blk(x_sb, m), op=ALU.add).then_inc(s.ready, 1)
                    return
                after(dve.tensor_tensor(tot[:, :], low[:, :], agg[:, 0:F], op=ALU.add), s.agg_free, m + 2)
                dve.wait_ge(s.own_z, m + 1)
                after(dve.tensor_tensor(own0, psM[:, 0:F], bias[:, 2, :], op=ALU.add), s.own_b, m + 1)
                after(dve.tensor_tensor(tot[:, :], tot[:, :], own0, op=ALU.add), s.tot, m + 1)
                after(dve.scalar_tensor_tensor(out=blk(x_sb, m), in0=tot[:, :], scalar=0.0, in1=blk(x_sb, m),
                                               op0=ALU.max, op1=ALU.add), s.x, m + 1, apart=True)
                after(dve.bn_stats(st1[:, :], blk(x_sb, m)), s.bn, m + 1, apart=True)
                after(dve.bn_aggr(mv1[:, :], st1[:, :]), s.var, m + 1)
                dve.wait_ge(s.std, m + 1)
                after(dve.reciprocal(rstd1[:, :], std1[:, :]), s.rstd, m + 1)
                dve.tensor_scalar(xn[:, 0, :], blk(x_sb, m), mv1[:, 0:1], rstd1[:, :],
                                  op0=ALU.subtract, op1=ALU.mult).then_inc(s.xn, 1)
                dve.wait_ge(s.hi, m + 1)
                after(dve.tensor_tensor(rest[:, 0, 0, :], psZ[0][:, 0:F], row_out[:, k, 0, 0, :], op=ALU.subtract),
                      s.rest, m + 1)
                dve.wait_ge(s.mid, m + 1)
                dve.tensor_tensor(row_out[:, k, 0, 2, :], rest[:, 0, 0, :], row_out[:, k, 0, 1, :],
                                  op=ALU.subtract).then_inc(s.ready, 1)

            def fast(l):
                s = L[l]
                dve.sem_inc(s.agg_free, 1)
                dve.sem_inc(s.hot[1], 1)
                dve.tensor_copy(base[:, :], base_0[:, :]).then_inc(s.based, 1)
                make_hot(l, 0, 0, None)
                own_normalise(l, 0)

                def step(m, k):
                    if is_there(m + 1):
                        make_hot(l, m + 1, m + 1, None)
                    finish(l, m, k)
                    if is_there(m + 1):
                        own_normalise(l, m + 1)
                in_pairs(dve, step)

            def general(l):
                s = L[l]
                dve.sem_inc(s.agg_free, 1)
                dve.sem_inc(s.hot[1], 1)
                dve.memset(base[:, :], 0.0).then_inc(s.based, 1)
                with dve.Fori(0, NB // 2) as g:
                    with dve.Fori(0, NB // 2) as i:
                        for k in range(2):
                            make_hot(l, g * NB + i * 2 + k, i * 2 + k, g)
                    dve.tensor_scalar(base[:, :], base[:, :], float(W2), None, op0=ALU.add).then_inc(s.based, 1)
                    for k in range(2):
                        own_normalise(l, g * 2 + k)
                        finish(l, g * 2 + k, k)

            for l in range(2):
                if l == 1:
                    dve.wait_ge(L[0].own, NB)
                either_path(dve, lambda: fast(l), lambda: general(l))


_INS = ["x", "src", "dst", "edge_type_2", "L0_gnn_W_data", "L0_gnn_b_data", "L0_gnn_W_control", "L0_gnn_b_control",
        "L0_gnn_W_self", "L0_gnn_b_self", "L1_gnn_W_in", "L1_gnn_W_out"]


def kernel(**inputs):
    import numpy as _np
    import concourse.bacc as _bacc
    from concourse import mybir as _mybir
    from concourse.bass_utils import run_bass_kernel_spmd as _run

    nc = _bacc.Bacc("TRN2", target_bir_lowering=False, num_devices=1)
    arrays, args = {}, []
    for name in _INS:
        a = _np.ascontiguousarray(inputs[name])
        arrays[f"in_{name}_dram"] = a
        args.append(nc.dram_tensor(f"in_{name}_dram", a.shape, _mybir.dt.from_np(a.dtype), kind="ExternalInput").ap())
    out = nc.dram_tensor("out_dram", inputs["x"].shape, _mybir.dt.float32, kind="ExternalOutput").ap()
    gnn_kernel(nc, *args, out)
    r = _run(nc, [arrays], core_ids=[0])
    return r.results[0]["out_dram"]
```

```python
import concourse.bass as bass
from concourse import mybir
from contextlib import ExitStack

P = 128



def gnn_kernel(nc, x, src, dst, etype, w_data, b_data, w_ctrl, b_ctrl, w_self, b_self, w_in, w_out, out):
    fp32, bf16, i32 = mybir.dt.float32, mybir.dt.bfloat16, mybir.dt.int32
    ALU, ACT, AX = mybir.AluOpType, mybir.ActivationFunctionType, mybir.AxisListType
    EPS = 1e-5

    N, F = x.shape
    E = src.shape[0]
    assert F == P
    NB = -(-N // P)
    LAST = N - (NB - 1) * P
    TPB = -(-E // N)
    T = NB * TPB
    assert NB % 2 == 0 and NB >= 4 and T * P >= E
    NPAD = NB * P
    HALVES = ((0, (TPB + 1) // 2), ((TPB + 1) // 2, TPB))
    TA = HALVES[0][1]
    PARTS = 3
    RW = PARTS * F
    RC = RW + 1
    RS = RC + 1
    W2 = 2 * P
    TYPES = (2, 1)
    FAR = float(2 ** 20)

    CH = -(-T // P)
    FULL = E // P
    REM = E - FULL * P
    FCH = FULL // P
    XTRA = FULL - FCH * P
    PAD_NODE = NPAD
    PIECES = 16 * ((FCH > 0) + (XTRA > 0) + (REM > 0))
    REAL = -(-E // P) - (NB - 1) * TPB
    assert TA < REAL <= TPB
    GROUPS = 4
    XCH = min(7, NB // 2)
    XB = [NB * c // XCH for c in range(XCH + 1)]

    DUOS = NB // 2
    RING = max(r for r in range(1, 8) if DUOS % r == 0)

    tables = [nc.dram_tensor(f"table{l}", (NPAD, RW), bf16, kind="Internal").ap() for l in range(2)]

    ctx = ExitStack()
    with ctx:
        def sb(name, shape, dt):
            return ctx.enter_context(nc.sbuf_tensor(name, shape, dt))

        def pb(name, shape, dt=fp32):
            return ctx.enter_context(nc.psum_tensor(name, shape, dt))

        def sem(name):
            return ctx.enter_context(nc.semaphore(name))

        x_sb = sb("x_sb", [P, NB * F], fp32)
        idx = sb("idx", [P, T], fp32)
        dst_f = sb("dst_f", [P, T], fp32)
        typed = sb("typed", [P, T], fp32)
        row_words = (TPB * RS + 1) // 2
        hot_words = TPB * 2 * W2 // 2
        arena = sb("arena", [P, max(row_words + hot_words, 4 * CH * P)], fp32)
        rows = arena[:, 0:row_words].bitcast(bf16)[:, 0:TPB * RS].rearrange("p (t c) -> p t c", c=RS)
        hot = arena[:, row_words:row_words + hot_words].bitcast(bf16).rearrange("p (t y c) -> p t y c", y=2, c=W2)
        raw = [arena[:, a * CH * P:(a + 1) * CH * P] for a in range(3)]
        raw_i = [r.bitcast(i32) for r in raw]
        bases = arena[:, 3 * CH * P:4 * CH * P]

        idx_now = sb("idx_now", [P, 2, TPB], i32)
        base = sb("base", [P, TPB], fp32)
        base_0 = sb("base_0", [P, TPB], fp32)
        rel = sb("rel", [P, TPB], fp32)
        rel_t = sb("rel_t", [P, TPB, 2], fp32)
        ident = sb("ident", [P, P], fp32)
        ones = sb("ones", [P, 1], fp32)
        zeros = sb("zeros", [P, RC], bf16)
        eps = sb("eps", [P, 1], fp32)
        iota = sb("iota", [P, W2], fp32)
        w_raw = sb("w_raw", [P, 5, F], fp32)
        wT = sb("wT", [P, 5, F], fp32)
        bias = sb("bias", [P, 3, F], fp32)
        stats = sb("stats", [P, NB * 6], fp32)
        mean2 = sb("mean2", [P, NB], fp32)
        var = sb("var", [P, NB], fp32)

        def stat_col(c):
            return stats[:, :].rearrange("p (n c) -> p n c", c=6)[:, :, c]
        std = sb("std", [P, NB], fp32)
        rstd = sb("rstd", [P, NB], fp32)
        shift = sb("shift", [P, NB], fp32)
        root = sb("root", [P, 1], fp32)
        tmax = sb("tmax", [P, CH], fp32)
        tmin = sb("tmin", [P, CH], fp32)
        missed = sb("missed", [P, 1], fp32)
        covered = sb("covered", [1, 1], i32)
        h = sb("h", [P, RING, 2, F], fp32)
        rest = sb("rest", [P, RING, 2, F], fp32)
        row_out = sb("row_out", [P, RING, 2, PARTS, F], bf16)
        agg = sb("agg", [P, 2, RC], fp32)
        low = sb("low", [P, 2, F], fp32)
        S = sb("S", [P, 2, F], fp32)
        ST = sb("ST", [P, 2, P], fp32)
        own_xn = sb("own_xn", [P, F], fp32)
        own_hT = sb("own_hT", [P, P], fp32)
        tot = sb("tot", [P, F], fp32)
        res = sb("res", [P, 2, F], fp32)
        st1 = sb("st1", [P, 6], fp32)
        mv1 = sb("mv1", [P, 2], fp32)
        std1 = sb("std1", [P, 1], fp32)
        rstd1 = sb("rstd1", [P, 1], fp32)

        bank = [[pb(f"bank{y}{k}", [P, 512]) for k in range(2)] for y in range(2)]
        psT = pb("psT", [P, 512])
        psZ = pb("psZ", [P, 512])
        psO = pb("psO", [P, 512])
        iota_ps = pb("iota_ps", [P, 512])
        turned = [psT, psZ, psO, bank[0][0], bank[0][1]]
        centre = bank[1][0]

        def blk(t, n):
            return t[:, bass.ds(n * F, F)]

        def col(t, n):
            return t[:, bass.ds(n, 1)]

        s_edges = [sem(f"s_edges_{a}") for a in ("dst", "type", "src")]
        s_w = sem("s_w")
        s_x = [sem(f"s_x{c}") for c in range(XCH)]
        s_pads = sem("s_pads")
        s_const = sem("s_const")
        s_ident = sem("s_ident")
        s_bases = sem("s_bases")
        s_float = [sem(f"s_float_{a}") for a in ("dst", "type", "src")]
        s_wt = sem("s_wt")
        s_wtc = sem("s_wtc")
        s_tr = sem("s_tr")
        s_trc = sem("s_trc")
        s_root = sem("s_root")
        s_iota = sem("s_iota")
        s_extent = sem("s_extent")
        s_centre = sem("s_centre")
        s_far = sem("s_far")
        s_missed = sem("s_missed")
        s_missum = sem("s_missum")
        s_covered = sem("s_covered")
        s_one = sem("s_one")
        s_bn = sem("s_bn")
        s_mean = sem("s_mean")
        s_var = sem("s_var")
        s_std = sem("s_std")
        s_rstd = sem("s_rstd")
        s_shift = sem("s_shift")
        s_xn = sem("s_xn")
        s_h = sem("s_h")
        s_hi = sem("s_hi")
        s_rest = sem("s_rest")
        s_mid = sem("s_mid")
        s_low = sem("s_low")
        s_st0 = [sem(f"s_st0{k}") for k in range(RING)]
        s_st1 = [sem(f"s_st1{k}") for k in range(2)]
        s_out = [sem(f"s_out{k}") for k in range(2)]

        class Layer:
            pass

        L = []
        for l in range(2):
            s = Layer()
            s.staged = sem(f"l{l}_staged")
            s.gathered = [sem(f"l{l}_gathered{h}") for h in "AB"]
            s.gathered_last = [[sem(f"l{l}_gathered_last{h}{g}") for g in range(GROUPS)] for h in "AB"]
            s.based = sem(f"l{l}_based")
            s.rel = sem(f"l{l}_rel")
            s.rel_t = sem(f"l{l}_rel_t")
            s.hot = [sem(f"l{l}_hot{h}") for h in "AB"]
            s.used = [sem(f"l{l}_used{h}") for h in "AB"]
            s.evac = sem(f"l{l}_evac")
            s.agg_free = sem(f"l{l}_agg_free")
            s.low = sem(f"l{l}_low")
            s.S = sem(f"l{l}_S")
            s.ST = sem(f"l{l}_ST")
            s.STc = sem(f"l{l}_STc")
            s.own_xn = sem(f"l{l}_own_xn")
            s.own_T = sem(f"l{l}_own_T")
            s.own_h = sem(f"l{l}_own_h")
            s.z = sem(f"l{l}_z")
            s.tot = sem(f"l{l}_tot")
            s.bn = sem(f"l{l}_bn")
            s.var = sem(f"l{l}_var")
            s.std = sem(f"l{l}_std")
            s.rstd = sem(f"l{l}_rstd")
            s.shift = sem(f"l{l}_shift")
            s.h = sem(f"l{l}_h")
            s.hi = sem(f"l{l}_hi")
            s.rest = sem(f"l{l}_rest")
            s.mid = sem(f"l{l}_mid")
            s.ready = sem(f"l{l}_ready")
            s.rfree = sem(f"l{l}_rfree")
            L.append(s)
        s_apart = {nc.gpsimd.engine: sem("s_apart_pool"), nc.vector.engine: sem("s_apart_dve")}

        block = ctx.enter_context(nc.Block())

        def in_duos(eng, step):
            rounds = DUOS // RING
            for j in range(RING):
                step(j, 0, j)
            if rounds > 2:
                with eng.Fori(1, rounds - 1) as i:
                    for j in range(RING):
                        step(i * RING + j, i, j)
            if rounds > 1:
                for j in range(RING):
                    step((rounds - 1) * RING + j, rounds - 1, j)

        def in_pairs(eng, step):
            step(0, 0)
            step(1, 1)
            if NB > 4:
                with eng.Fori(1, NB // 2 - 1) as i:
                    for k in range(2):
                        step(i * 2 + k, k)
            step(NB - 2, 0)
            step(NB - 1, 1)

        def is_there(n):
            return not isinstance(n, int) or 0 <= n < NB

        def tiles_of(hf, seq):
            a, b = HALVES[hf]
            return (a, min(b, REAL)) if isinstance(seq, int) and seq == NB - 1 else (a, b)

        def in_groups(hf, seq):
            return isinstance(seq, int) and (seq == NB - 1 or (seq, hf) == (NB - 2, 1))

        def group_of(hf, t):
            a, b = HALVES[hf]
            return (t - a) * GROUPS // (b - a)

        def wait_apart(eng, semaphore, n):
            eng.wait_ge(semaphore, n)
            eng.sem_inc(s_apart[eng.engine], 1)

        def either_path(eng, fast, general):
            eng.wait_ge(s_covered, 1)
            with eng.If(eng.value_load(covered[0:1, 0:1], min_val=0, max_val=1) == 1):
                fast()
            with eng.Else():
                general()

        @block.sync
        def _(sp):
            for l in range(2):
                sp.sem_inc(L[l].rfree, 2)
            sp.wait_ge(s_pads, 4)
            for a, lst in enumerate((dst, etype, src)):
                if FCH:
                    sp.dma_start(raw_i[a][:, 0:FCH * P].rearrange("p (c e) -> p c e", e=P),
                                 lst[0:FCH * P * P].rearrange("(c p e) -> p c e", p=P, e=P)).then_inc(s_edges[a], 16)
                if XTRA:
                    sp.dma_start(raw_i[a][0:XTRA, FCH * P:FCH * P + P],
                                 lst[FCH * P * P:FULL * P].rearrange("(p e) -> p e", e=P)).then_inc(s_edges[a], 16)
                if REM:
                    sp.dma_start(raw_i[a][XTRA:XTRA + 1, FCH * P:FCH * P + REM],
                                 lst[FULL * P:E].rearrange("(p e) -> p e", p=1)).then_inc(s_edges[a], 16)
            for c in range(XCH):
                n0, n1 = XB[c], min(XB[c + 1], NB - 1)
                sp.dma_start(x_sb[:, n0 * F:n1 * F].rearrange("p (n f) -> p n f", f=F),
                             x[n0 * P:n1 * P, :].rearrange("(n p) f -> p n f", p=P)).then_inc(s_x[c], 16)
            sp.dma_start(x_sb[0:LAST, (NB - 1) * F:NB * F], x[(NB - 1) * P:N, :]).then_inc(s_x[XCH - 1], 16)

            def store_duo(d, i, j):
                sp.wait_ge(s_low, d + 1)
                sp.dma_start(tables[0][bass.ds(d * (2 * P), 2 * P), :].rearrange("(n p) c -> p n c", p=P),
                             row_out[:, j, :, :, :].rearrange("p n a f -> p n (a f)")).then_inc(s_st0[j], 16)
            in_duos(sp, store_duo)

            def store(l, m, k):
                s = L[l]
                sp.wait_ge(s.ready, m + 1)
                done = (s_st1, s_out)[l]
                if l == 0:
                    sp.dma_start(tables[1][bass.ds(m * P, P), :],
                                 row_out[:, 0, k, :, :].rearrange("p a f -> p (a f)")).then_inc(done[k], 16)
                elif isinstance(m, int) and m == NB - 1:
                    sp.dma_start(out[m * P:N, :], res[0:LAST, k, :]).then_inc(done[k], 16)
                else:
                    sp.dma_start(out[bass.ds(m * P, P), :], res[:, k, :]).then_inc(done[k], 16)
                if k == 1:
                    for j in range(2):
                        sp.wait_ge(done[j], (m - 1) * 8 + 16)
                        sp.sem_inc(s.rfree, 1)

            for l in range(2):
                in_pairs(sp, lambda m, k: store(l, m, k))
            for k in range(2):
                sp.wait_ge(s_out[k], 16 * (NB // 2))

        @block.gpsimd
        def _(pool):
            for a, v in enumerate((PAD_NODE, 0, 0)):
                pool.memset(raw_i[a][:, FCH * P:CH * P], v).then_inc(s_pads, 1)
            pool.memset(x_sb[:, (NB - 1) * F:NB * F], 0.0).then_inc(s_pads, 1)
            pool.memset(ident[:, :], 0.0).then_inc(s_ident, 1)
            pool.memset(ones[:, :], 1.0).then_inc(s_const, 1)
            pool.memset(zeros[:, :], 0.0).then_inc(s_const, 1)
            pool.memset(eps[:, :], EPS).then_inc(s_const, 1)
            pool.wait_ge(s_ident, 1)
            pool.affine_select(out=ident[:, :], in_=ident[:, :], compare_op=ALU.not_equal, fill=1.0,
                               base=0, pattern=[[-1, P]], channel_multiplier=1).then_inc(s_ident, 1)
            pool.iota(iota[:, :], [[1, W2]], base=0, channel_multiplier=0,
                      allow_small_or_imprecise_dtypes=True).then_inc(s_const, 1)
            for hf, (a, b) in enumerate(HALVES):
                pool.iota(base_0[:, a:b], [[0, b - a]], base=(hf - 1) * P, channel_multiplier=0,
                          allow_small_or_imprecise_dtypes=True).then_inc(s_const, 1)
                pool.iota(bases[:, 0:T].rearrange("p (n t) -> p n t", t=TPB)[:, :, a:b], [[P, NB], [0, b - a]],
                          base=(hf - 1) * P, channel_multiplier=0,
                          allow_small_or_imprecise_dtypes=True).then_inc(s_bases, 1)
            pool.memset(bases[:, T:CH * P], float((NB - 1) * P)).then_inc(s_bases, 1)

            def split(d, i, j):
                pool.wait_ge(s_hi, d + 1)
                pool.tensor_tensor(rest[:, j, :, :], h[:, j, :, :], row_out[:, j, :, 0, :],
                                   op=ALU.subtract).then_inc(s_rest, 1)
            in_duos(pool, split)
            for j in range(RING):
                pool.wait_ge(s_st0[j], 16 * (DUOS // RING))

            def gather(l, seq, k):
                s = L[l]
                wait_apart(pool, s.staged, seq + 1)
                for hf in range(2):
                    wait_apart(pool, s.used[hf], seq + 1 + hf)
                    for t in range(*tiles_of(hf, seq)):
                        done = s.gathered_last[hf][group_of(hf, t)] if in_groups(hf, seq) else s.gathered[hf]
                        pool.indirect_dma_start(
                            out=rows[:, t, 0:RW], out_offset=None, in_=tables[l],
                            in_offset=bass.IndirectOffsetOnAxis(ap=idx_now[:, k, t:t + 1], axis=0),
                            compute_op=ALU.bypass).then_inc(done, 16)

            def general(l):
                with pool.Fori(0, NB // 2) as g:
                    with pool.Fori(0, NB // 2) as i:
                        for k in range(2):
                            gather(l, g * NB + i * 2 + k, k)

            for l in range(2):
                if l == 1:
                    for k in range(2):
                        pool.wait_ge(s_st1[k], 16 * (NB // 2))
                either_path(pool, lambda: in_pairs(pool, lambda n, k: gather(l, n, k)), lambda: general(l))

        @block.tensor
        def _(pe):
            pe.wait_ge(s_ident, 2)
            pe.wait_ge(s_w, 16 * 8)
            for j in range(5):
                pe.transpose(turned[j][:, 0:P], w_raw[:, j, :], ident[:, :]).then_inc(s_wt, 1)
            pe.wait_ge(s_wtc, 5)
            g = 0
            for a in (0, 2, 1):
                pe.wait_ge(s_float[a], 1)
                for c0 in range(0, CH, 4):
                    if g >= 4:
                        pe.wait_ge(s_trc, g - 3)
                    for c in range(c0, min(c0 + 4, CH)):
                        last = pe.transpose(turned[g % 4][:, (c - c0) * P:(c - c0 + 1) * P],
                                            raw[a][:, c * P:(c + 1) * P], ident[:, :])
                    last.then_inc(s_tr, 1)
                    g += 1
            pe.wait_ge(s_bases, 3)
            pe.wait_ge(s_const, 6)
            for c in range(CH):
                last = pe.matmul(centre[:, c:c + 1], bases[0:1, c * P:(c + 1) * P], ones[0:1, 0:1],
                                 start=(c == 0), stop=(c == CH - 1), skip_group_check=True)
            last.then_inc(s_centre, 1)
            pe.wait_ge(s_missed, 1)
            pe.matmul(centre[0:1, 0:1], missed[:, :], ones[:, :], start=True, stop=True).then_inc(s_missum, 1)

            def add_rows(l, seq, hf, to, fresh=None):
                s = L[l]
                pe.wait_ge(s.hot[hf], seq + 1 + hf)
                if fresh is not None:
                    pe.wait_ge(s.evac, fresh)
                a, b = tiles_of(hf, seq)
                if not in_groups(hf, seq):
                    pe.wait_ge(s.gathered[hf], seq * (16 * (b - a)) + 16 * (b - a))
                for t in range(a, b):
                    g = group_of(hf, t)
                    if in_groups(hf, seq) and (t == a or group_of(hf, t - 1) < g):
                        pe.wait_ge(s.gathered_last[hf][g],
                                   16 * sum(group_of(hf, u) == g for n in range(NB - 2, seq + 1)
                                            if in_groups(hf, n) for u in range(*tiles_of(hf, n))))
                    for w in range(2):
                        for y in range(TYPES[l]):
                            last = pe.matmul(bank[y][to[w]][:, 0:RC], hot[:, t, y, w * P:(w + 1) * P],
                                             rows[:, t, 0:RC], start=(w == 1 and fresh is not None and t == a),
                                             stop=False, skip_group_check=True)
                last.then_inc(s.used[hf], 1)

            def finish(l, m):
                s = L[l]
                pe.wait_ge(s.own_xn, m + 1)
                pe.transpose(psO[:, 0:P], own_xn[:, :], ident[:, :]).then_inc(s.own_T, 1)
                pe.wait_ge(s.S, m + 1)
                for y in range(TYPES[l]):
                    last = pe.transpose(psT[:, y * P:(y + 1) * P], S[:, y, :], ident[:, :])
                last.then_inc(s.ST, 1)
                pe.wait_ge(s.own_h, m + 1)
                if l == 0:
                    pe.matmul(psZ[:, 0:F], own_hT[:, :], wT[:, 2, :], start=True, stop=False)
                else:
                    pe.matmul(psO[:, 0:F], own_hT[:, :], wT[:, 4, :], start=True, stop=True)
                pe.wait_ge(s.STc, m + 1)
                if l == 0:
                    pe.matmul(psZ[:, 0:F], ST[:, 0, :], wT[:, 0, :], start=False, stop=False)
                    pe.matmul(psZ[:, 0:F], ST[:, 1, :], wT[:, 1, :], start=False, stop=True).then_inc(s.z, 1)
                else:
                    pe.matmul(psZ[:, 0:F], ST[:, 0, :], wT[:, 3, :], start=True, stop=True).then_inc(s.z, 1)

            def open_banks(l):
                for y in range(TYPES[l]):
                    for k in range(2):
                        pe.matmul(bank[y][k][:, 0:RC], zeros[:, 0:P], zeros[:, :], start=True, stop=False,
                                  skip_group_check=True)

            def begin(l):
                pe.wait_ge(s_one, 1)
                pe.wait_ge(s_iota, 2)
                if l == 1:
                    pe.wait_ge(L[0].evac, NB + 1)
                for hf in range(2):
                    pe.sem_inc(L[l].used[hf], 1 + hf)

            def fast(l):
                begin(l)
                open_banks(l)
                add_rows(l, 0, 0, (1, 0))

                def step(m, k):
                    if not is_there(m + 1):
                        finish(l, m - 1)
                    add_rows(l, m, 1, (k, 1 - k), fresh=m + 1)
                    if is_there(m + 1):
                        if is_there(m - 1):
                            finish(l, m - 1)
                        add_rows(l, m + 1, 0, (k, 1 - k))
                in_pairs(pe, step)
                finish(l, NB - 1)

            def general(l):
                s = L[l]
                begin(l)
                with pe.Fori(0, NB // 2) as g:
                    pe.wait_ge(s.evac, g * 2 + 1)
                    open_banks(l)
                    with pe.Fori(0, NB // 2) as i:
                        for k in range(2):
                            for hf in range(2):
                                add_rows(l, g * NB + i * 2 + k, hf, (0, 1))
                    for k in range(2):
                        finish(l, g * 2 + k)

            for l in range(2):
                either_path(pe, lambda: fast(l), lambda: general(l))

        @block.scalar
        def _(act):
            for j, w in enumerate((w_data, w_ctrl, w_self, w_in, w_out)):
                act.dma_start(w_raw[:, j, :], w).then_inc(s_w, 16)
            for j, b in enumerate((b_data, b_ctrl, b_self)):
                act.dma_start(bias[:, j, :], b.rearrange("(a f) -> a f", a=1).partition_broadcast(P)).then_inc(s_w, 16)
            act.wait_ge(s_const, 6)
            act.activation(root[:, :], eps[:, :], ACT.Sqrt).then_inc(s_root, 1)
            for j in range(5):
                act.wait_ge(s_wt, j + 1)
                act.activation(wT[:, j, :], turned[j][:, 0:P], ACT.Copy).then_inc(s_wtc, 1)
            act.wait_ge(s_edges[2], PIECES)
            act.activation(raw[2], raw_i[2], ACT.Copy).then_inc(s_float[2], 1)
            g = 0
            for to in (dst_f, idx, typed):
                for c0 in range(0, CH, 4):
                    act.wait_ge(s_tr, g + 1)
                    n = min(T, (c0 + 4) * P) - c0 * P
                    act.activation(to[:, c0 * P:c0 * P + n], turned[g % 4][:, 0:n], ACT.Copy).then_inc(s_trc, 1)
                    g += 1
            act.wait_ge(s_var, 1)
            act.activation(std[:, :], var[:, :], ACT.Sqrt, bias=eps[:, :], scale=1.0 / F).then_inc(s_std, 1)

            def relu(d, j):
                act.wait_ge(s_xn, d + 1)
                act.activation(h[:, j, :, :], h[:, j, :, :], ACT.Relu).then_inc(s_h, 1)

            def high(d, i, j):
                if not isinstance(i, int) or i > 0:
                    act.wait_ge(s_st0[j], i * 16)
                act.wait_ge(s_h, d + 1)
                act.activation(row_out[:, j, :, 0, :], h[:, j, :, :], ACT.Copy).then_inc(s_hi, 1)

            def middle(d, i, j):
                ahead = not isinstance(d, int) or d + 2 < DUOS
                if ahead:
                    relu(d + 2, (j + 2) % RING)
                act.wait_ge(s_rest, d + 1)
                act.activation(row_out[:, j, :, 1, :], rest[:, j, :, :], ACT.Copy).then_inc(s_mid, 1)
                if ahead:
                    high(d + 2, i + (j + 2) // RING, (j + 2) % RING)
            for d in range(2):
                relu(d, d)
                high(d, 0, d)
            in_duos(act, middle)

            def stage(l, seq, n, k):
                s = L[l]
                if not isinstance(seq, int) or seq >= 2:
                    act.wait_ge(s.used[1], seq + 1)
                act.activation(idx_now[:, k, :], idx[:, bass.ds(n * TPB, TPB)], ACT.Copy).then_inc(s.staged, 1)

            def evacuate(l, m, k):
                s = L[l]
                act.wait_ge(s.agg_free, m + 1)
                for y in range(TYPES[l]):
                    last = act.activation(agg[:, y, :], bank[y][k][:, 0:RC], ACT.Copy)
                last.then_inc(s.evac, 1)

            def finish(l, m, k):
                s = L[l]
                act.wait_ge(s.own_T, m + 1)
                act.activation(own_hT[:, :], psO[:, 0:P], ACT.Relu).then_inc(s.own_h, 1)
                act.wait_ge(s.ST, m + 1)
                act.activation(ST[:, 0:TYPES[l], :], psT[:, 0:TYPES[l] * P].rearrange("p (y f) -> p y f", f=P),
                               ACT.Copy).then_inc(s.STc, 1)
                if l == 1:
                    return
                act.wait_ge(s.var, m + 1)
                act.activation(std1[:, :], mv1[:, 1:2], ACT.Sqrt, bias=eps[:, :]).then_inc(s.std, 1)
                act.wait_ge(s.shift, m + 1)
                act.activation(h[:, 0, 0, :], blk(x_sb, m), ACT.Relu, bias=col(shift, m), scale=rstd1[:, :]).then_inc(s.h, 1)
                act.wait_ge(s.rfree, m + 1)
                act.wait_ge(s.h, m + 1)
                act.activation(row_out[:, 0, k, 0, :], h[:, 0, 0, :], ACT.Copy).then_inc(s.hi, 1)
                act.wait_ge(s.rest, m + 1)
                act.activation(row_out[:, 0, k, 1, :], rest[:, 0, 0, :], ACT.Copy).then_inc(s.mid, 1)

            def fast(l):
                s = L[l]
                act.sem_inc(s.evac, 1)
                stage(l, 0, 0, 0)
                stage(l, 1, 1, 1)

                def step(m, k):
                    if is_there(m + 2):
                        stage(l, m + 2, m + 2, k)
                    if is_there(m - 1):
                        finish(l, m - 1, 1 - k)
                    if is_there(m + 1):
                        act.wait_ge(s.used[0], m + 3)
                    else:
                        act.wait_ge(s.used[1], NB + 2)
                    evacuate(l, m, k)
                in_pairs(act, step)
                finish(l, NB - 1, 1)

            def general(l):
                s = L[l]
                act.sem_inc(s.evac, 1)
                with act.Fori(0, NB // 2) as g:
                    with act.Fori(0, NB // 2) as i:
                        for k in range(2):
                            stage(l, g * NB + i * 2 + k, i * 2 + k, k)
                    act.wait_ge(s.used[1], g * NB + NB + 2)
                    for k in range(2):
                        evacuate(l, g * 2 + k, k)
                        finish(l, g * 2 + k, k)

            for l in range(2):
                either_path(act, lambda: fast(l), lambda: general(l))

        @block.vector
        def _(dve):
            def after(ins, semaphore, n, apart=False):
                ins.then_inc(semaphore, 1)
                if apart:
                    wait_apart(dve, semaphore, n)
                else:
                    dve.wait_ge(semaphore, n)

            dve.wait_ge(s_const, 6)
            dve.tensor_copy(iota_ps[:, 0:W2], iota[:, :]).then_inc(s_iota, 1)
            dve.tensor_scalar(iota_ps[:, W2:2 * W2], iota[:, :], -FAR, None, op0=ALU.add).then_inc(s_iota, 1)
            dve.wait_ge(s_edges[0], PIECES)
            after(dve.tensor_copy(raw[0], raw_i[0]), s_float[0], 1)
            dst_tiles = raw[0].rearrange("p (c e) -> p c e", e=P)
            dve.tensor_reduce(tmax[:, :], dst_tiles, axis=AX.X, op=ALU.max).then_inc(s_extent, 1)
            dve.tensor_reduce(tmin[:, :], dst_tiles, axis=AX.X, op=ALU.min).then_inc(s_extent, 1)
            dve.wait_ge(s_edges[1], PIECES)
            dve.tensor_scalar(raw[1], raw_i[1], 0.0, FAR, op0=ALU.not_equal, op1=ALU.mult).then_inc(s_float[1], 1)

            for c in range(XCH):
                dve.wait_ge(s_x[c], 32 if c == XCH - 1 else 16)
                for n in range(XB[c], XB[c + 1]):
                    dve.bn_stats(stats[:, n * 6:(n + 1) * 6], blk(x_sb, n)).then_inc(s_bn, 1)
            dve.wait_ge(s_bn, NB)
            dve.tensor_tensor(mean2[:, :], stat_col(1), stat_col(4), op=ALU.add).then_inc(s_mean, 1)
            after(dve.tensor_tensor(var[:, :], stat_col(1), stat_col(4), op=ALU.subtract), s_mean, 2)
            after(dve.tensor_tensor(var[:, :], var[:, :], var[:, :], op=ALU.mult), s_mean, 3)
            after(dve.scalar_tensor_tensor(out=var[:, :], in0=var[:, :], scalar=F / 4.0, in1=stat_col(2),
                                           op0=ALU.mult, op1=ALU.add), s_mean, 4)
            dve.tensor_tensor(var[:, :], var[:, :], stat_col(5), op=ALU.add).then_inc(s_var, 1)
            dve.wait_ge(s_std, 1)
            after(dve.reciprocal(rstd[:, :], std[:, :]), s_rstd, 1)
            after(dve.scalar_tensor_tensor(out=shift[:, :], in0=mean2[:, :], scalar=-0.5, in1=rstd[:, :],
                                           op0=ALU.mult, op1=ALU.mult), s_shift, 1)

            def normalise(to, n):
                return dve.tensor_scalar(to, blk(x_sb, n), col(rstd, n), col(shift, n), op0=ALU.mult, op1=ALU.add)

            def normalise_duo(d, j):
                for k in range(2):
                    last = normalise(h[:, j, k, :], d * 2 + k)
                last.then_inc(s_xn, 1)

            AHEAD = min(4, RING)

            def lowest(d, i, j):
                dve.wait_ge(s_mid, d + 1)
                dve.tensor_tensor(row_out[:, j, :, 2, :], rest[:, j, :, :], row_out[:, j, :, 1, :],
                                  op=ALU.subtract).then_inc(s_low, 1)
                if not isinstance(d, int) or d + AHEAD < DUOS:
                    normalise_duo(d + AHEAD, (j + AHEAD) % RING)
            for d in range(AHEAD):
                normalise_duo(d, d)
            in_duos(dve, lowest)
            dve.wait_ge(s_extent, 2)
            dve.wait_ge(s_centre, 1)
            dve.tensor_tensor(tmax[:, :], tmax[:, :], centre[:, 0:CH], op=ALU.subtract).then_inc(s_far, 1)
            after(dve.tensor_tensor(tmin[:, :], tmin[:, :], centre[:, 0:CH], op=ALU.subtract), s_far, 2)
            after(dve.tensor_scalar(tmax[:, :], tmax[:, :], W2 - 0.5, None, op0=ALU.is_gt), s_far, 3)
            after(dve.scalar_tensor_tensor(out=tmin[:, :], in0=tmin[:, :], scalar=-0.5, in1=tmax[:, :],
                                           op0=ALU.is_lt, op1=ALU.add), s_far, 4)
            dve.tensor_reduce(missed[:, :], tmin[:, :], axis=AX.X, op=ALU.add).then_inc(s_missed, 1)
            dve.wait_ge(s_trc, 3 * -(-CH // 4))
            dve.memset(rows[:, :, RW:RS], 1.0).then_inc(s_one, 1)
            dve.wait_ge(s_missum, 1)
            after(dve.tensor_scalar(covered[0:1, 0:1], centre[0:1, 0:1], 0.0, None, op0=ALU.is_equal), s_covered, 1)

            def relate(l, seq, n, moves=None):
                s = L[l]
                dve.wait_ge(s.based, (seq if moves is None else moves) + 1)
                dve.wait_ge(s.hot[1], seq + 1)
                after(dve.tensor_tensor(rel[:, :], dst_f[:, bass.ds(n * TPB, TPB)], base[:, :], op=ALU.subtract),
                      s.rel, seq + 1)
                if moves is None:
                    dve.tensor_scalar(base[:, :], base[:, :], float(P), None, op0=ALU.add).then_inc(s.based, 1)
                if l == 0:
                    dve.tensor_tensor(rel_t[:, :, 0], rel[:, :], typed[:, bass.ds(n * TPB, TPB)], op=ALU.add)
                    after(dve.tensor_tensor(rel_t[:, :, 1], rel[:, :], typed[:, bass.ds(n * TPB, TPB)],
                                            op=ALU.subtract), s.rel_t, seq + 1)

            def make_hot(l, seq, hf):
                s = L[l]
                a, b = tiles_of(hf, seq)
                dve.wait_ge(s.used[hf], seq + 1 + hf)
                if l == 0:
                    shape = [P, b - a, 2, W2]
                    made = dve.tensor_tensor(
                        hot[:, a:b, :, :],
                        iota_ps[:, :].rearrange("p (y c) -> p y c", y=2).unsqueeze(1).to_broadcast(shape),
                        rel_t[:, a:b, :].unsqueeze(3).to_broadcast(shape), op=ALU.is_equal)
                else:
                    shape = [P, b - a, W2]
                    made = dve.tensor_tensor(hot[:, a:b, 0, :], iota_ps[:, 0:W2].unsqueeze(1).to_broadcast(shape),
                                             rel[:, a:b].unsqueeze(2).to_broadcast(shape), op=ALU.is_equal)
                made.then_inc(s.hot[hf], 1)

            def sum_parts(l, m):
                s = L[l]
                y = TYPES[l]
                dve.wait_ge(s.evac, m + 2)
                after(dve.tensor_tensor(low[:, 0:y, :], agg[:, 0:y, F:2 * F], agg[:, 0:y, 2 * F:3 * F], op=ALU.add),
                      s.low, m + 1)
                dve.tensor_tensor(S[:, 0:y, :], low[:, 0:y, :], agg[:, 0:y, 0:F], op=ALU.add).then_inc(s.S, 1)
                normalise(own_xn[:, :], m).then_inc(s.own_xn, 1)

            def finish(l, m, k):
                s = L[l]
                dve.wait_ge(s.z, m + 1)
                if l == 1:
                    after(dve.tensor_tensor(tot[:, :], psZ[:, 0:F], blk(x_sb, m), op=ALU.add), s.tot, m + 1)
                    dve.wait_ge(s.rfree, m + 1)
                    after(dve.scalar_tensor_tensor(out=res[:, k, :], in0=psO[:, 0:F], scalar=agg[:, 0, RW:RC],
                                                   in1=tot[:, :], op0=ALU.mult, op1=ALU.add), s.ready, m + 1)
                    dve.sem_inc(s.agg_free, 1)
                    return
                after(dve.scalar_tensor_tensor(out=tot[:, :], in0=bias[:, 0, :], scalar=agg[:, 0, RW:RC],
                                               in1=psZ[:, 0:F], op0=ALU.mult, op1=ALU.add), s.tot, m * 3 + 1)
                after(dve.scalar_tensor_tensor(out=tot[:, :], in0=bias[:, 1, :], scalar=agg[:, 1, RW:RC],
                                               in1=tot[:, :], op0=ALU.mult, op1=ALU.add), s.agg_free, m + 2)
                after(dve.tensor_tensor(tot[:, :], tot[:, :], bias[:, 2, :], op=ALU.add), s.tot, m * 3 + 2)
                after(dve.scalar_tensor_tensor(out=blk(x_sb, m), in0=tot[:, :], scalar=0.0, in1=blk(x_sb, m),
                                               op0=ALU.max, op1=ALU.add), s.tot, m * 3 + 3, apart=True)
                after(dve.bn_stats(st1[:, :], blk(x_sb, m)), s.bn, m + 1, apart=True)
                after(dve.bn_aggr(mv1[:, :], st1[:, :]), s.var, m + 1)
                dve.wait_ge(s.std, m + 1)
                after(dve.reciprocal(rstd1[:, :], std1[:, :]), s.rstd, m * 2 + 1)
                dve.tensor_scalar(col(shift, m), mv1[:, 0:1], rstd1[:, :], -1.0,
                                  op0=ALU.mult, op1=ALU.mult).then_inc(s.shift, 1)
                dve.tensor_copy(col(rstd, m), rstd1[:, :]).then_inc(s.rstd, 1)
                dve.wait_ge(s.hi, m + 1)
                after(dve.tensor_tensor(rest[:, 0, 0, :], h[:, 0, 0, :], row_out[:, 0, k, 0, :], op=ALU.subtract),
                      s.rest, m + 1)
                dve.wait_ge(s.mid, m + 1)
                dve.tensor_tensor(row_out[:, 0, k, 2, :], rest[:, 0, 0, :], row_out[:, 0, k, 1, :],
                                  op=ALU.subtract).then_inc(s.ready, 1)

            def fast(l):
                s = L[l]
                dve.sem_inc(s.agg_free, 1)
                dve.sem_inc(s.hot[1], 1)
                dve.tensor_copy(base[:, :], base_0[:, :]).then_inc(s.based, 1)
                relate(l, 0, 0)
                make_hot(l, 0, 0)
                make_hot(l, 0, 1)
                relate(l, 1, 1)
                make_hot(l, 1, 0)

                def step(m, k):
                    if is_there(m - 1):
                        finish(l, m - 1, 1 - k)
                    if is_there(m + 1):
                        make_hot(l, m + 1, 1)
                    sum_parts(l, m)
                    if is_there(m + 2):
                        relate(l, m + 2, m + 2)
                        make_hot(l, m + 2, 0)
                in_pairs(dve, step)
                finish(l, NB - 1, 1)

            def general(l):
                s = L[l]
                dve.sem_inc(s.agg_free, 1)
                dve.sem_inc(s.hot[1], 1)
                dve.memset(base[:, :], 0.0).then_inc(s.based, 1)
                with dve.Fori(0, NB // 2) as g:
                    with dve.Fori(0, NB // 2) as i:
                        for k in range(2):
                            relate(l, g * NB + i * 2 + k, i * 2 + k, g)
                            make_hot(l, g * NB + i * 2 + k, 0)
                            make_hot(l, g * NB + i * 2 + k, 1)
                    dve.tensor_scalar(base[:, :], base[:, :], float(W2), None, op0=ALU.add).then_inc(s.based, 1)
                    for k in range(2):
                        sum_parts(l, g * 2 + k)
                        finish(l, g * 2 + k, k)

            for l in range(2):
                either_path(dve, lambda: fast(l), lambda: general(l))


_INS = ["x", "src", "dst", "edge_type_2", "L0_gnn_W_data", "L0_gnn_b_data", "L0_gnn_W_control", "L0_gnn_b_control",
        "L0_gnn_W_self", "L0_gnn_b_self", "L1_gnn_W_in", "L1_gnn_W_out"]


def kernel(**inputs):
    import numpy as _np
    import concourse.bacc as _bacc
    from concourse import mybir as _mybir
    from concourse.bass_utils import run_bass_kernel_spmd as _run

    nc = _bacc.Bacc("TRN2", target_bir_lowering=False, num_devices=1)
    arrays, args = {}, []
    for name in _INS:
        a = _np.ascontiguousarray(inputs[name])
        arrays[f"in_{name}_dram"] = a
        args.append(nc.dram_tensor(f"in_{name}_dram", a.shape, _mybir.dt.from_np(a.dtype), kind="ExternalInput").ap())
    out = nc.dram_tensor("out_dram", inputs["x"].shape, _mybir.dt.float32, kind="ExternalOutput").ap()
    gnn_kernel(nc, *args, out)
    r = _run(nc, [arrays], core_ids=[0])
    return r.results[0]["out_dram"]
```
